# Optimizing a Trainium2 kernel written in Bass

```python
import numpy as np
import jax
import jax.numpy as jnp

def _softmax(x, axis=-1):
    return jax.nn.softmax(x, axis=axis)

def _gelu(x):
    return jax.nn.gelu(x, approximate=True)

def _silu(x):
    return jax.nn.silu(x)

def _sigmoid(x):
    return jax.nn.sigmoid(x)

def _layernorm(x, axis=-1, eps=1e-05):
    m = jnp.mean(x, axis=axis, keepdims=True)
    v = jnp.var(x, axis=axis, keepdims=True)
    return (x - m) / jnp.sqrt(v + eps)

def _scatter_add(tgt, idx, src, axis=0):
    return tgt.at[idx].add(src)

def _segment_sum(src, seg, n):
    return jax.ops.segment_sum(src, seg, n)
kernel_name = 'mk_flamingo_gated_d1_seqx_r2_960585'

def setup_inputs(seed: int=0):
    np.random.seed(seed)
    _w = jnp.asarray

    def _rec_inputs():
        import jax
        import jax.numpy as jnp
        _rk = jax.random.key(seed)
        x = 0.0003765 + 1 * jax.random.normal(jax.random.fold_in(_rk, 1), (8, 512, 1024), jnp.float32)
        _lenS = 512 - jax.random.randint(jax.random.fold_in(_rk, 7), (8,), 0, max(1, 512 // 4) + 1, jnp.int32)
        _lenS2 = 512 - jax.random.randint(jax.random.fold_in(_rk, 8), (8,), 0, max(1, 512 // 4) + 1, jnp.int32)
        _ctx_2048P = jax.random.normal(jax.random.fold_in(_rk, 11), (8, 16, 1024), jnp.float32)
        _ctx_2048c = jax.random.dirichlet(jax.random.fold_in(_rk, 511), 0.3 * jnp.ones((16,), jnp.float32), (8, 512))
        _ctx_2048t = jnp.einsum('bsk,bkd->bsd', _ctx_2048c, _ctx_2048P)
        _ctx_2048t = _ctx_2048t * jax.lax.rsqrt(jnp.mean(jnp.square(_ctx_2048t)) + 1e-12) * 0.953939
        ctx_2048 = -0.000292821 + 1.00034 * (_ctx_2048t + 0.3 * jax.random.normal(jax.random.fold_in(_rk, 611), (8, 512, 1024), jnp.float32))
        _g = jax.random.normal(jax.random.fold_in(_rk, 9001), (2, 1), jnp.float32)
        _g = jnp.sign(_g) * jnp.maximum(jnp.abs(_g), 1.0) + (_g == 0) * 1.0
        g_xattn = _g[0]
        g_ffn = _g[1]
        return (x, ctx_2048, g_xattn, g_ffn)
    x, ctx_2048, g_xattn, g_ffn = _rec_inputs()

    def _L0_xattn_setup():
        import jax, jax.numpy as jnp
        import numpy as np
        key = jax.random.key(seed)
        k1, k2, k3, k4, k5 = jax.random.split(key, 5)
        B, D_MODEL, L = (2, 512, 1024)
        HEAD_DIM = 8
        H = D_MODEL // HEAD_DIM
        return {'k': jax.random.normal(k1, (B, D_MODEL, L), dtype=jnp.float32), 'v': jax.random.normal(k2, (B, D_MODEL, L), dtype=jnp.float32), 'q': jax.random.normal(k3, (B, D_MODEL, L), dtype=jnp.float32), 'ssm_kernel': jax.random.normal(k4, (H, L), dtype=jnp.float32), 'D': jax.random.normal(k5, (H,), dtype=jnp.float32), 'head_dim': HEAD_DIM}
    _L0_xattn_all = _L0_xattn_setup()
    _L0_xattn_in = {k: v for k, v in _L0_xattn_all.items() if k in ('ssm_kernel', 'D')}
    del _L0_xattn_all

    def _L0_ffn_setup():
        import jax, jax.numpy as jnp
        import numpy as np
        B, S, H = (4, 1024, 1024)
        E = 8
        F = H // E
        TOPK = 2
        LORA_R = 16
        LORA_SCALE = 1.0
        key = jax.random.key(seed)
        ks = jax.random.split(key, 7)
        x = jax.random.normal(ks[0], (B, S, H), dtype=jnp.float32)
        G = jax.random.normal(ks[1], (H, E), dtype=jnp.float32)
        gate_w = jax.random.normal(ks[2], (E, F, H), dtype=jnp.float32) * np.float32(np.sqrt(2.0 / H))
        up_w = jax.random.normal(ks[3], (E, F, H), dtype=jnp.float32) * np.float32(np.sqrt(2.0 / H))
        down_w = jax.random.normal(ks[4], (E, H, F), dtype=jnp.float32) * np.float32(np.sqrt(2.0 / F))
        lora_A = jax.random.normal(ks[5], (E, LORA_R, H), dtype=jnp.float32) * np.float32(np.sqrt(2.0 / H))
        lora_B = jax.random.normal(ks[6], (E, H, LORA_R), dtype=jnp.float32) * np.float32(np.sqrt(2.0 / LORA_R))
        return {'x': x, 'G': G, 'gate_w': gate_w, 'up_w': up_w, 'down_w': down_w, 'lora_A': lora_A, 'lora_B': lora_B}
    _L0_ffn_all = _L0_ffn_setup()
    _L0_ffn_in = {k: v for k, v in _L0_ffn_all.items() if k in ('G', 'gate_w', 'up_w', 'down_w', 'lora_A', 'lora_B')}
    del _L0_ffn_all
    return {'x': x, 'ctx_2048': ctx_2048, 'g_xattn': g_xattn, 'g_ffn': g_ffn, 'L0_xattn_ssm_kernel': _L0_xattn_in['ssm_kernel'], 'L0_xattn_D': _L0_xattn_in['D'], 'L0_ffn_G': _L0_ffn_in['G'], 'L0_ffn_gate_w': _L0_ffn_in['gate_w'], 'L0_ffn_up_w': _L0_ffn_in['up_w'], 'L0_ffn_down_w': _L0_ffn_in['down_w'], 'L0_ffn_lora_A': _L0_ffn_in['lora_A'], 'L0_ffn_lora_B': _L0_ffn_in['lora_B']}

def reference(x, ctx_2048, g_xattn, g_ffn, L0_xattn_ssm_kernel, L0_xattn_D, L0_ffn_G, L0_ffn_gate_w, L0_ffn_up_w, L0_ffn_down_w, L0_ffn_lora_A, L0_ffn_lora_B):
    import jax
    import jax.numpy as jnp

    def _L0_xattn_ref(k, v, q, ssm_kernel, D, head_dim):
        import jax, jax.numpy as jnp
        import numpy as np
        B, HD, L = k.shape
        H = HD // head_dim
        fft_size = 2 * L
        k_ = k.reshape(B, H, head_dim, L)
        v_ = v.reshape(B, H, head_dim, L)
        q_ = q.reshape(B, H, head_dim, L)
        kv = jnp.einsum('bhil,bhjl->bijhl', k_, v_)
        kv_f = jnp.fft.rfft(kv, n=fft_size)
        kernel_f = jnp.fft.rfft(ssm_kernel, n=fft_size)
        y = jnp.fft.irfft(kv_f * kernel_f, n=fft_size)[..., :L]
        out = y + kv * D[None, None, None, :, None]
        out = jnp.einsum('bijhl,bhil->bjhl', out, q_)
        out = jnp.transpose(out, (0, 2, 1, 3)).reshape(B, H * head_dim, L)
        return out.astype(k.dtype)

    def _L0_ffn_ref(x, G, gate_w, up_w, down_w, lora_A, lora_B):
        import jax, jax.numpy as jnp
        import numpy as np
        B, S, H = (4, 1024, 1024)
        E = 8
        F = H // E
        TOPK = 2
        LORA_R = 16
        LORA_SCALE = 1.0
        scores = jax.nn.softmax(jnp.einsum('bsh,he->bse', x, G), axis=-1)
        value, indices = jax.lax.top_k(scores, TOPK)
        onehot = jax.nn.one_hot(indices, E, dtype=value.dtype)
        w = jnp.einsum('bsk,bske->bse', value, onehot)
        gate = jax.nn.silu(jnp.einsum('bsh,efh->bsef', x, gate_w))
        up = jnp.einsum('bsh,efh->bsef', x, up_w)
        gated = gate * up
        out = jnp.einsum('bsef,bse,ehf->bsh', gated, w, down_w)
        lr = jnp.einsum('bsh,erh->bser', x, lora_A)
        out = out + LORA_SCALE * jnp.einsum('bser,bse,ehr->bsh', lr, w, lora_B)
        return out
    x = x + jnp.tanh(g_xattn[0]) * _L0_xattn_ref(ctx_2048, ctx_2048, _layernorm(x, axis=-1), L0_xattn_ssm_kernel, L0_xattn_D, 8)
    x = x + jnp.tanh(g_ffn[0]) * _L0_ffn_ref(_layernorm(x, axis=-1), L0_ffn_G, L0_ffn_gate_w, L0_ffn_up_w, L0_ffn_down_w, L0_ffn_lora_A, L0_ffn_lora_B)
    return x

_drawn_inputs = setup_inputs


def setup_inputs(seed=0):
    import zlib

    import numpy as np

    out = dict(_drawn_inputs(seed))
    spreads = {}
    factors = {}
    for name, (base, spread) in spreads.items():
        noise = np.random.default_rng([zlib.crc32(name.encode()), seed]).standard_normal(out[name].shape)
        drawn = base * np.exp(spread * noise) if base else spread * noise
        out[name] = jnp.asarray(drawn.astype(out[name].dtype))
    for name, factor in factors.items():
        out[name] = (out[name] * factor).astype(out[name].dtype)
    return out
```

```python
from contextlib import ExitStack

import concourse.bass as bass
from concourse import mybir

F32 = mybir.dt.float32
F32R = mybir.dt.float32r
ALU = mybir.AluOpType
ACT = mybir.ActivationFunctionType
AX = mybir.AxisListType

P = 128
B, CH, L = 8, 512, 1024
HD = 8
NH = CH // HD
HT = 2
CT = HT * HD
NT = CH // CT
NC = L // P
IB = HD * B
WR = IB + IB // 2
ND = 4
YC = ND * IB + IB // 2
FULL = ND * IB
SK = IB + B
ZS = 9
ZC = ZS * IB
ZB = 5 * IB
ZE = 8 * IB
KW = L + P
NP = NC // 2
EPS = 1e-5

E, F, R = 8, 128, 16
TG = 8
NG = NT // TG
TOK = TG * P
HALF = 512
NS = E + 1


def view(ap, dims, shift=0):
    return bass.AP(tensor=ap.tensor, offset=ap.offset + shift, ap=[list(ap.ap[0])] + [list(d) for d in dims])


def stage1(nc, x_d, c_d, k_d, dskip_d, g_d, ident_d, kpad_d, x1_d):
    ctx = ExitStack()
    with ctx:
        sb = lambda n, s, dt=F32: ctx.enter_context(nc.sbuf_tensor(n, s, dt))
        sem = lambda n: ctx.enter_context(nc.semaphore(n))
        x_nat = [sb(f"x_nat{p}", [P, L]) for p in range(2)]
        x_new = [sb(f"x_new{p}", [P, L]) for p in range(2)]
        xn = sb("xn", [P, L])
        cT = [sb(f"cT{p}", [P, HT, NC, WR]) for p in range(2)]
        qT = [sb(f"qT{p}", [P, HT, NC, WR]) for p in range(2)]
        kv = [sb(f"kv{h}", [P, NC, YC]) for h in range(HT)]
        kvhi = [sb(f"kvhi{h}", [P, NC, YC], F32R) for h in range(HT)]
        kvlo = [sb(f"kvlo{h}", [P, NC, YC], F32R) for h in range(HT)]
        t_raw = [sb(f"t_raw{h}", [P, L]) for h in range(HT)]
        t_hi = [sb(f"t_hi{h}", [P, L], F32R) for h in range(HT)]
        t_lo = [sb(f"t_lo{h}", [P, L], F32R) for h in range(HT)]
        oT = [sb(f"oT{p}", [P, NC, P]) for p in range(2)]
        z = [sb(f"z{p}", [P, 2, ZC]) for p in range(2)]
        ident = sb("ident", [P, P])
        krow = sb("krow", [NH, KW])
        dcol = sb("dcol", [NH, 1])
        gate = sb("gate", [P, 1])
        gt = sb("gt", [P, 1])
        epsc = sb("epsc", [P, 1])
        st = sb("st", [P, 2, 6])
        mv = sb("mv", [P, 2])
        sd = sb("sd", [P, 1])
        rs = sb("rs", [P, 1])
        Y = [ctx.enter_context(nc.psum_tensor(f"Y{s}", [P, 2, HALF], F32)) for s in range(2)]
        OP = ctx.enter_context(nc.psum_tensor("OP", [P, L], F32))
        XP = ctx.enter_context(nc.psum_tensor("XP", [P, L], F32))

        const_in = sem("const_in")
        k_in = sem("k_in")
        k_sum = sem("k_sum")
        k_out = sem("k_out")
        gate_ready = sem("gate_ready")
        x_in = [sem(f"x_in{p}") for p in range(2)]
        c_in = [sem(f"c_in{p}") for p in range(2)]
        t_in = [sem(f"t_in{h}") for h in range(HT)]
        thi_done = sem("thi_done")
        tlo_done = sem("tlo_done")
        kv_done = sem("kv_done")
        kvhi_done = sem("kvhi_done")
        kvlo_done = sem("kvlo_done")
        y_ready = sem("y_ready")
        z_done = sem("z_done")
        z_zero = sem("z_zero")
        sum_done = sem("sum_done")
        o_ready = sem("o_ready")
        res_done = sem("res_done")
        x_out = [sem(f"x_out{p}") for p in range(2)]
        st_done = sem("st_done")
        sd_done = sem("sd_done")
        xn_done = sem("xn_done")
        xt_ready = sem("xt_ready")
        q_done = sem("q_done")

        def kernel_window(n):
            return bass.AP(tensor=kpad_d.tensor, offset=n * KW, ap=[[1, P], [1, L]])

        with nc.Block() as block:

            @block.sync
            def _(eng):
                eng.dma_start(krow[:], k_d).then_inc(k_in, 16)
                eng.dma_start(dcol[:], dskip_d).then_inc(k_in, 16)
                eng.dma_start(x_nat[0][:], x_d[0]).then_inc(x_in[0], 16)
                eng.dma_start(cT[0][:], c_d[0]).then_inc(c_in[0], 16)
                eng.dma_start(ident[:], ident_d).then_inc(const_in, 16)
                eng.dma_start(gate[:], g_d).then_inc(const_in, 16)
                eng.wait_ge(k_sum, 1)
                eng.dma_start(kpad_d, krow[:]).then_inc(k_out, 16)
                eng.dma_start(cT[1][:], c_d[1]).then_inc(c_in[1], 16)
                eng.wait_ge(k_out, 16)
                for h in range(HT):
                    eng.dma_start(t_raw[h][:], kernel_window(h)).then_inc(t_in[h], 16)

                def body(i, p, first=False, last=False):
                    if not last:
                        for h in range(HT):
                            eng.wait_ge(thi_done, 2 * i + h + 1)
                            eng.wait_ge(tlo_done, 2 * i + h + 1)
                            eng.dma_start(t_raw[h][:], kernel_window(2 * i + 2 + h)).then_inc(t_in[h], 16)
                    if not first:
                        eng.wait_ge(res_done, i)
                    if not last:
                        eng.dma_start(x_nat[1 - p][:], x_d[i + 1]).then_inc(x_in[1 - p], 16)
                    if not first:
                        eng.dma_start(x1_d[i - 1], x_new[1 - p][:]).then_inc(x_out[1 - p], 16)
                        if not last:
                            eng.wait_ge(kv_done, 4 * i)
                            eng.dma_start(cT[1 - p][:], c_d[i + 1]).then_inc(c_in[1 - p], 16)

                body(0, 0, first=True)
                body(1, 1)
                with eng.Fori(1, NT // 2 - 1) as k:
                    for p in range(2):
                        body(2 * k + p, p)
                body(NT - 2, 0)
                body(NT - 1, 1, last=True)
                eng.wait_ge(res_done, NT)
                eng.dma_start(x1_d[NT - 1], x_new[1][:]).then_inc(x_out[1], 16)
                for p in range(2):
                    eng.wait_ge(x_out[p], 16 * (NT // 2))

            @block.gpsimd
            def _(eng):
                def products(n, h, half, i, p, have):
                    eng.wait_ge(c_in[p], have)
                    if not (isinstance(n, int) and n < HT):
                        eng.wait_ge(kvhi_done, 2 * (n - HT) + half + 1)
                        eng.wait_ge(kvlo_done, 2 * (n - HT) + half + 1)
                    c0 = half * (NC // 2)
                    cc = cT[p][:, h, c0:c0 + NC // 2, 0:IB]
                    o = kv[h][:, c0:c0 + NC // 2, 0:IB]
                    nc.gpsimd.tensor_tensor(view(o, [[YC, NC // 2], [IB, ND], [1, IB]]),
                                            view(cc, [[WR, NC // 2], [0, ND], [1, IB]]),
                                            view(cc, [[WR, NC // 2], [B, ND], [1, IB]]), ALU.mult)
                    nc.gpsimd.tensor_tensor(kv[h][:, c0:c0 + NC // 2, FULL:YC],
                                            cT[p][:, h, c0:c0 + NC // 2, 0:IB // 2],
                                            cT[p][:, h, c0:c0 + NC // 2, IB // 2:IB], ALU.mult).then_inc(kv_done, 1)

                def low(n, h):
                    eng.wait_ge(thi_done, n + 1)
                    nc.gpsimd.tensor_tensor(t_lo[h][:], t_raw[h][:], t_hi[h][:].bitcast(F32),
                                            ALU.subtract).then_inc(tlo_done, 1)

                def low_and_normal(n, h, i, p):
                    eng.wait_ge(st_done, 3 * i + 3)
                    if not (isinstance(i, int) and i < 1):
                        eng.wait_ge(xt_ready, i)
                    low(n, h)
                    nc.gpsimd.tensor_scalar(xn[:], x_nat[p][:], mv[:, 0:1], rs[:, 0:1], ALU.subtract,
                                            ALU.mult).then_inc(xn_done, 1)

                products(0, 0, 0, 0, 0, 16)
                products(0, 0, 1, 0, 0, 16)
                low_and_normal(0, 0, 0, 0)

                def body(i, p, k, last=False):
                    products(2 * i + 1, 1, 0, i, p, 16 * (k + 1))
                    products(2 * i + 1, 1, 1, i, p, 16 * (k + 1))
                    low(2 * i + 1, 1)
                    if not last:
                        products(2 * i + 2, 0, 0, i + 1, 1 - p, 16 * (k + 1 + p))
                        products(2 * i + 2, 0, 1, i + 1, 1 - p, 16 * (k + 1 + p))
                        low_and_normal(2 * i + 2, 0, i + 1, 1 - p)

                body(0, 0, 0)
                body(1, 1, 0)
                with eng.Fori(1, NT // 2 - 1) as k:
                    for p in range(2):
                        body(2 * k + p, p, k)
                body(NT - 2, 0, NT // 2 - 1)
                body(NT - 1, 1, NT // 2 - 1, last=True)

            @block.scalar
            def _(eng):
                def high_t(n, h, have):
                    eng.wait_ge(t_in[h], have)
                    if not (isinstance(n, int) and n < HT):
                        eng.wait_ge(y_ready, NP * (n - 1))
                    nc.scalar.copy(t_hi[h][:], t_raw[h][:]).then_inc(thi_done, 1)

                def high_kv(n, h):
                    for half in range(2):
                        eng.wait_ge(kv_done, 2 * n + half + 1)
                        if half == 0 and not (isinstance(n, int) and n < HT):
                            eng.wait_ge(y_ready, NP * (n - 1))
                        c0 = half * (NC // 2)
                        nc.scalar.copy(kvhi[h][:, c0:c0 + NC // 2, :],
                                       kv[h][:, c0:c0 + NC // 2, :]).then_inc(kvhi_done, 1)

                def root(i):
                    eng.wait_ge(st_done, 3 * i + 2)
                    nc.scalar.activation(sd[:], mv[:, 1:2], ACT.Sqrt, bias=epsc[:, 0:1]).then_inc(sd_done, 1)

                def take_q(i, p):
                    eng.wait_ge(xt_ready, i + 1)
                    if not (isinstance(i, int) and i < 2):
                        eng.wait_ge(z_done, 8 * (i - 1))
                    src = XP[:]
                    nc.scalar.copy(qT[p][:, :, :, 0:IB], view(src, [[IB, HT], [P, NC], [1, IB]]))
                    nc.scalar.copy(qT[p][:, :, :, IB:WR], view(src, [[IB, HT], [P, NC], [1, IB // 2]])) \
                        .then_inc(q_done, 1)

                eng.wait_ge(const_in, 32)
                nc.scalar.activation(gt[:], gate[:], ACT.Tanh).then_inc(gate_ready, 1)
                root(0)
                high_t(0, 0, 16)
                high_kv(0, 0)
                take_q(0, 0)

                def body(i, p, k, last=False):
                    high_t(2 * i + 1, 1, 16 * (i + 1))
                    high_kv(2 * i + 1, 1)
                    if not last:
                        root(i + 1)
                        high_t(2 * i + 2, 0, 16 * (i + 2))
                        high_kv(2 * i + 2, 0)
                        take_q(i + 1, 1 - p)

                body(0, 0, 0)
                body(1, 1, 0)
                with eng.Fori(1, NT // 2 - 1) as k:
                    for p in range(2):
                        body(2 * k + p, p, k)
                body(NT - 2, 0, NT // 2 - 1)
                body(NT - 1, 1, NT // 2 - 1, last=True)

            @block.vector
            def _(eng):
                def multiply(i, p, h, r):
                    s = r % 2
                    idx = 8 * i + 4 * h + r
                    eng.wait_ge(y_ready, idx + 1)
                    if h == 0 and r == 0:
                        eng.wait_ge(q_done, i + 1)
                    if not (isinstance(i, int) and i == 0 and h == 0 and r < 2):
                        eng.wait_ge(sum_done, idx - 1)
                    y = Y[s][:, :, 0:YC]
                    q = qT[p][:, h, 2 * r:2 * r + 2, :]
                    zz = z[s][:]
                    nc.vector.tensor_tensor(view(zz, [[ZC, 2], [SK, ND], [1, IB]]),
                                            view(y, [[HALF, 2], [IB, ND], [1, IB]]),
                                            view(q, [[WR, 2], [0, ND], [1, IB]]), ALU.mult)
                    nc.vector.tensor_tensor(view(zz, [[ZC, 2], [IB, ND - 1], [1, IB]], ZB),
                                            view(y, [[HALF, 2], [IB, ND - 1], [1, IB]], IB),
                                            view(q, [[WR, 2], [B, ND - 1], [1, IB]], B), ALU.mult)
                    nc.vector.tensor_tensor(view(zz, [[ZC, 2], [IB // 2, 2], [1, IB // 2]], ZE),
                                            view(y, [[HALF, 2], [0, 2], [1, IB // 2]], FULL),
                                            view(q, [[WR, 2], [IB // 2, 2], [1, IB // 2]], IB // 2),
                                            ALU.mult).then_inc(z_done, 1)

                def total(i, p, h, r):
                    s = r % 2
                    eng.wait_ge(z_done, 8 * i + 4 * h + r + 1)
                    if h == 0 and r == 0 and not (isinstance(i, int) and i < 2):
                        eng.wait_ge(o_ready, i - 1)
                    nc.vector.tensor_reduce(oT[p][:, 2 * r:2 * r + 2, h * IB:(h + 1) * IB],
                                            view(z[s][:], [[ZC, 2], [1, IB], [IB, ZS]]), AX.X,
                                            ALU.add).then_inc(sum_done, 1)

                def low_kv(n, h, half):
                    eng.wait_ge(kvhi_done, 2 * n + half + 1)
                    c0 = half * (NC // 2)
                    nc.vector.tensor_tensor(kvlo[h][:, c0:c0 + NC // 2, :], kv[h][:, c0:c0 + NC // 2, :],
                                            kvhi[h][:, c0:c0 + NC // 2, :].bitcast(F32),
                                            ALU.subtract).then_inc(kvlo_done, 1)

                def stats(i, p, have):
                    eng.wait_ge(x_in[p], have)
                    if not (isinstance(i, int) and i < 1):
                        eng.wait_ge(xn_done, i)
                    nc.vector.bn_stats(st[:, 0, :], x_nat[p][:, 0:HALF])
                    nc.vector.bn_stats(st[:, 1, :], x_nat[p][:, HALF:L]).then_inc(st_done, 1)

                def aggregate(i):
                    nc.vector.bn_aggr(mv[:], st[:].rearrange("p a b -> p (a b)")).then_inc(st_done, 1)

                def invert(i):
                    eng.wait_ge(sd_done, i + 1)
                    nc.vector.reciprocal(rs[:], sd[:]).then_inc(st_done, 1)

                def residual(i, p):
                    eng.wait_ge(o_ready, i + 1)
                    if not (isinstance(i, int) and i < 2):
                        eng.wait_ge(x_out[p], stored[p](i))
                    nc.vector.scalar_tensor_tensor(out=x_new[p][:], in0=OP[:], scalar=gt[:, 0:1],
                                                   in1=x_nat[p][:], op0=ALU.mult,
                                                   op1=ALU.add).then_inc(res_done, 1)

                stored = [lambda i: 8 * i, lambda i: 8 * i - 8]

                nc.vector.memset(epsc[:], EPS)
                nc.vector.memset(z[0][:], 0.0)
                nc.vector.memset(z[1][:], 0.0).then_inc(z_zero, 1)
                eng.wait_ge(k_in, 32)
                nc.vector.tensor_tensor(krow[:, P - 1:P], krow[:, P - 1:P], dcol[:], ALU.add).then_inc(k_sum, 1)
                eng.wait_ge(z_zero, 1)
                stats(0, 0, 16)
                eng.wait_ge(st_done, 1)
                aggregate(0)
                invert(0)
                low_kv(0, 0, 0)
                low_kv(0, 0, 1)
                eng.wait_ge(gate_ready, 1)

                def body(i, p, k, first=False, last=False):
                    multiply(i, p, 0, 0)
                    if not first:
                        total(i - 1, 1 - p, 1, 3)
                    low_kv(2 * i + 1, 1, 0)
                    multiply(i, p, 0, 1)
                    total(i, p, 0, 0)
                    low_kv(2 * i + 1, 1, 1)
                    multiply(i, p, 0, 2)
                    total(i, p, 0, 1)
                    if not first:
                        residual(i - 1, 1 - p)
                    multiply(i, p, 0, 3)
                    total(i, p, 0, 2)
                    if not last:
                        stats(i + 1, 1 - p, 16 * (k + 1 + p))
                    multiply(i, p, 1, 0)
                    if not last:
                        eng.wait_ge(st_done, 3 * i + 4)
                    total(i, p, 0, 3)
                    if not last:
                        aggregate(i + 1)
                    multiply(i, p, 1, 1)
                    if not last:
                        invert(i + 1)
                    total(i, p, 1, 0)
                    if not last:
                        low_kv(2 * i + 2, 0, 0)
                    multiply(i, p, 1, 2)
                    total(i, p, 1, 1)
                    if not last:
                        low_kv(2 * i + 2, 0, 1)
                    multiply(i, p, 1, 3)
                    total(i, p, 1, 2)

                body(0, 0, 0, first=True)
                body(1, 1, 0)
                with eng.Fori(1, NT // 2 - 1) as k:
                    for p in range(2):
                        body(2 * k + p, p, k)
                body(NT - 2, 0, NT // 2 - 1)
                body(NT - 1, 1, NT // 2 - 1, last=True)
                total(NT - 1, 1, 1, 3)
                residual(NT - 1, 1)

            @block.tensor
            def _(eng):
                def conv(i, h, r):
                    n = 2 * i + h
                    idx = 8 * i + 4 * h + r
                    s2 = r % 2
                    if r == 0:
                        eng.wait_ge(tlo_done, n + 1)
                        eng.wait_ge(kvlo_done, 2 * n + 1)
                    if r == 2:
                        eng.wait_ge(kvlo_done, 2 * n + 2)
                    if not (isinstance(i, int) and i == 0 and h == 0 and r < 2):
                        eng.wait_ge(z_done, idx - 1)
                    for a in range(2):
                        c = 2 * r + a
                        for s in range(c + 1):
                            w = slice((c - s) * P, (c - s + 1) * P)
                            for t, m in ((t_hi, kvhi), (t_hi, kvlo), (t_lo, kvhi)):
                                mm = nc.tensor.matmul(Y[s2][:, a, 0:YC], t[h][:, w], m[h][:, s, :],
                                                      start=(s == 0 and t is t_hi and m is kvhi),
                                                      stop=(s == c and t is t_lo))
                    mm.then_inc(y_ready, 1)

                def transpose_x(i):
                    eng.wait_ge(xn_done, i + 1)
                    if not (isinstance(i, int) and i < 1):
                        eng.wait_ge(q_done, i)
                    for c in range(NC):
                        mm = nc.tensor.transpose(XP[:, c * P:(c + 1) * P], xn[:, c * P:(c + 1) * P], ident[:])
                    mm.then_inc(xt_ready, 1)

                def transpose_o(i, p):
                    eng.wait_ge(sum_done, 8 * i + 8)
                    if not (isinstance(i, int) and i < 1):
                        eng.wait_ge(res_done, i)
                    for c in range(NC):
                        mm = nc.tensor.transpose(OP[:, c * P:(c + 1) * P], oT[p][:, c, :], ident[:])
                    mm.then_inc(o_ready, 1)

                eng.wait_ge(const_in, 32)
                transpose_x(0)

                def body(i, p, first=False, last=False):
                    for r in range(NP):
                        conv(i, 0, r)
                        if r == 2 and not first:
                            transpose_o(i - 1, 1 - p)
                    for r in range(NP):
                        conv(i, 1, r)
                        if r == 2 and not last:
                            transpose_x(i + 1)

                body(0, 0, first=True)
                body(1, 1)
                with eng.Fori(1, NT // 2 - 1) as k:
                    for p in range(2):
                        body(2 * k + p, p)
                body(NT - 2, 0)
                body(NT - 1, 1, last=True)
                transpose_o(NT - 1, 1)


def stage2(nc, x1_d, gu_d, dn_d, la_d, lb_d, rg_d, g_d, ident_d, order_d, sel_d, out_d):
    ctx = ExitStack()
    with ctx:
        sb = lambda n, s, dt=F32: ctx.enter_context(nc.sbuf_tensor(n, s, dt))
        sem = lambda n: ctx.enter_context(nc.semaphore(n))
        ps = lambda n, s: ctx.enter_context(nc.psum_tensor(n, s, F32))
        xhi = sb("xhi", [P, NC, TOK], F32R)
        xlo = sb("xlo", [P, NC, TOK], F32R)
        y = sb("y", [P, TG, L])
        gu_raw = sb("gu_raw", [P, 2, NC, F])
        dn_raw = sb("dn_raw", [P, L])
        gu_hi = [sb(f"gu_hi{p}", [P, 2, NC, F], F32R) for p in range(2)]
        gu_lo = [sb(f"gu_lo{p}", [P, 2, NC, F], F32R) for p in range(2)]
        dn_hi = [sb(f"dn_hi{p}", [P, L], F32R) for p in range(2)]
        dn_lo = [sb(f"dn_lo{p}", [P, L], F32R) for p in range(2)]
        la_hi = sb("la_hi", [P, NC, E * R], F32R)
        la_lo = sb("la_lo", [P, NC, E * R], F32R)
        lb_hi = sb("lb_hi", [P, L], F32R)
        lb_lo = sb("lb_lo", [P, L], F32R)
        h = sb("h", [P, TOK])
        h_hi = [sb(f"h_hi{p}", [P, TOK], F32R) for p in range(2)]
        h_lo = [sb(f"h_lo{p}", [P, TOK], F32R) for p in range(2)]
        xs = [sb(f"xs{p}", [P, L]) for p in range(2)]
        wexp = sb("wexp", [P, TOK])
        ident = sb("ident2", [P, P])
        sel = sb("sel", [E, E * R])
        order = sb("order", [P, TG, E])
        rg = sb("rg", [P, NC, E])
        rg_hi = sb("rg_hi", [P, NC, E], F32R)
        rg_lo = sb("rg_lo", [P, NC, E], F32R)
        sc = sb("sc", [P, TG, E])
        ta = sb("ta", [P, TG, E])
        oh = sb("oh", [P, TG, E])
        w = sb("w", [P, TG, E])
        col = sb("col", [P, TG])
        gate = sb("gate2", [P, 1])
        gt = sb("gt2", [P, 1])
        epsc = sb("epsc2", [P, 1])
        st = sb("st2", [P, 2, 6])
        mv = sb("mv2", [P, 2])
        sd = sb("sd2", [P, 1])
        rs = sb("rs2", [P, 1])
        G = ps("G", [P, TOK])
        U = ps("U", [P, TOK])
        D = [ps(f"D{s}", [P, L]) for s in range(2)]
        tile_ps = [U, G]

        const_in = sem("const_in2")
        xs_in = [sem(f"xs_in{p}") for p in range(2)]
        st_done = sem("st_done2")
        sd_done = sem("sd_done2")
        xs_done = sem("xs_done")
        tr_done = sem("tr_done")
        xhi_done = sem("xhi_done")
        xlo_done = sem("xlo_done")
        lg_done = sem("lg_done")
        rt = sem("rt")
        ex_done = sem("ex_done")
        wt_done = sem("wt_done")
        wx_done = sem("wx_done")
        gu_in, dn_in, lora_in = sem("gu_in"), sem("dn_in"), sem("lora_in")
        guhi_done, gulo_done = sem("guhi_done"), sem("gulo_done")
        dnhi_done, dnlo_done = sem("dnhi_done"), sem("dnlo_done")
        lora_split = sem("lora_split")
        misc = sem("misc")
        g_ready = sem("g_ready")
        u_ready = sem("u_ready")
        silu_done = sem("silu_done")
        h_done = sem("h_done")
        hhi_done, hlo_done = sem("hhi_done"), sem("hlo_done")
        d_ready = sem("d_ready")
        acc_done = sem("acc_done")
        y_in, y_out = sem("y_in"), sem("y_out")
        RTS = 18

        with nc.Block() as block:

            @block.sync
            def _(eng):
                def load_x(t, n, T):
                    if not (isinstance(T, int) and T < 2):
                        eng.wait_ge(tr_done, T - 1)
                    eng.dma_start(xs[t % 2][:], x1_d[T]).then_inc(xs_in[t % 2], 16)

                def load_gu(m):
                    if not (isinstance(m, int) and m < 1):
                        eng.wait_ge(guhi_done, m)
                        eng.wait_ge(gulo_done, m)

                def load_dn(m):
                    if not (isinstance(m, int) and m < 1):
                        eng.wait_ge(dnhi_done, m)
                        eng.wait_ge(dnlo_done, m)

                eng.dma_start(ident[:], ident_d).then_inc(const_in, 16)
                eng.dma_start(gate[:], g_d).then_inc(const_in, 16)
                eng.dma_start(order[:], order_d).then_inc(const_in, 16)
                eng.dma_start(sel[:], sel_d).then_inc(const_in, 16)
                eng.dma_start(rg[:], rg_d).then_inc(const_in, 16)
                load_x(0, 0, 0)
                load_x(1, 0, 1)
                eng.dma_start(gu_raw[:, 0, :, :], la_d).then_inc(lora_in, 16)
                eng.dma_start(dn_raw[:], lb_d).then_inc(lora_in, 16)
                eng.wait_ge(lora_split, 4)
                eng.dma_start(gu_raw[:], gu_d[0]).then_inc(gu_in, 16)
                eng.dma_start(dn_raw[:], dn_d[0]).then_inc(dn_in, 16)
                for t in range(2, TG):
                    load_x(t, 0, t)
                for t in range(TG):
                    eng.dma_start(y[:, t, :], x1_d[t]).then_inc(y_in, 16)
                load_gu(1)
                eng.dma_start(gu_raw[:], gu_d[1]).then_inc(gu_in, 16)

                def steps(g, last=False):
                    for e in range(E):
                        if not (last and e >= E - 2):
                            load_gu(8 * g + e + 2)
                            eng.dma_start(gu_raw[:], gu_d[(e + 2) % E]).then_inc(gu_in, 16)
                        if not (last and e >= E - 1):
                            load_dn(8 * g + e + 1)
                            eng.dma_start(dn_raw[:], dn_d[(e + 1) % E]).then_inc(dn_in, 16)
                    for t in range(TG):
                        if not last:
                            load_x(t, 0, 8 * g + TG + t)
                        eng.wait_ge(acc_done, 72 * g + 64 + t + 1)
                        eng.dma_start(out_d[8 * g + t], y[:, t, :]).then_inc(y_out, 16)
                    if not last:
                        eng.wait_ge(y_out, 128 * g + 128)
                        for t in range(TG):
                            eng.dma_start(y[:, t, :], x1_d[8 * g + TG + t]).then_inc(y_in, 16)

                steps(0)
                with eng.Fori(1, NG - 1) as g:
                    steps(g)
                steps(NG - 1, last=True)
                eng.wait_ge(y_out, 16 * NT)

            @block.gpsimd
            def _(eng):
                eng.wait_ge(lora_split, 2)
                nc.gpsimd.tensor_tensor(la_lo[:], gu_raw[:, 0, :, :], la_hi[:].bitcast(F32),
                                        ALU.subtract).then_inc(lora_split, 1)
                nc.gpsimd.tensor_tensor(lb_lo[:], dn_raw[:], lb_hi[:].bitcast(F32),
                                        ALU.subtract).then_inc(lora_split, 1)

                def low_gu(m, p):
                    eng.wait_ge(guhi_done, m + 1)
                    nc.gpsimd.tensor_tensor(gu_lo[p][:], gu_raw[:], gu_hi[p][:].bitcast(F32),
                                            ALU.subtract).then_inc(gulo_done, 1)

                def low_dn(m, p):
                    eng.wait_ge(dnhi_done, m + 1)
                    nc.gpsimd.tensor_tensor(dn_lo[p][:], dn_raw[:], dn_hi[p][:].bitcast(F32),
                                            ALU.subtract).then_inc(dnlo_done, 1)

                low_gu(0, 0)
                low_dn(0, 0)
                low_gu(1, 1)

                def steps(g, last=False):
                    for e in range(E):
                        if not (last and e >= E - 2):
                            low_gu(8 * g + e + 2, e % 2)
                        if not (last and e >= E - 1):
                            low_dn(8 * g + e + 1, (e + 1) % 2)

                steps(0)
                with eng.Fori(1, NG - 1) as g:
                    steps(g)
                steps(NG - 1, last=True)

            @block.scalar
            def _(eng):
                def high_gu(m, p):
                    eng.wait_ge(gu_in, 16 * (m + 1))
                    nc.scalar.copy(gu_hi[p][:], gu_raw[:]).then_inc(guhi_done, 1)

                def high_dn(m, p):
                    eng.wait_ge(dn_in, 16 * (m + 1))
                    nc.scalar.copy(dn_hi[p][:], dn_raw[:]).then_inc(dnhi_done, 1)

                def tile_root(T):
                    eng.wait_ge(st_done, 3 * T + 2)
                    nc.scalar.activation(sd[:], mv[:, 1:2], ACT.Sqrt, bias=epsc[:, 0:1]).then_inc(sd_done, 1)

                def tile_high(t, T):
                    eng.wait_ge(tr_done, T + 1)
                    nc.scalar.copy(xhi[:, :, t * P:(t + 1) * P],
                                   tile_ps[t % 2][:].rearrange("p (c n) -> p c n", c=NC)).then_inc(xhi_done, 1)

                eng.wait_ge(const_in, 80)
                nc.scalar.activation(gt[:], gate[:], ACT.Tanh).then_inc(misc, 1)
                nc.scalar.copy(rg_hi[:], rg[:]).then_inc(misc, 1)
                eng.wait_ge(lora_in, 32)
                nc.scalar.copy(la_hi[:], gu_raw[:, 0, :, :]).then_inc(lora_split, 1)
                nc.scalar.copy(lb_hi[:], dn_raw[:]).then_inc(lora_split, 1)
                for t in range(TG):
                    tile_root(t)
                    if t:
                        tile_high(t - 1, t - 1)
                    if t == 1:
                        high_gu(0, 0)
                        high_dn(0, 0)
                tile_high(TG - 1, TG - 1)
                high_gu(1, 1)

                def steps(g, last=False):
                    for e in range(NS):
                        n = NS * g + e
                        if e == 0:
                            eng.wait_ge(rt, RTS * g + 2)
                            nc.scalar.activation(sc[:], sc[:], ACT.Exp).then_inc(ex_done, 1)
                        if e < E:
                            eng.wait_ge(g_ready, E * g + e + 1)
                            if not (isinstance(g, int) and g == 0 and e == 0):
                                eng.wait_ge(hlo_done, n)
                            nc.scalar.activation(h[:], G[:], ACT.Silu).then_inc(silu_done, 1)
                        eng.wait_ge(h_done, n + 1)
                        if not (isinstance(g, int) and g == 0 and e < 2):
                            eng.wait_ge(d_ready, TG * n if e == 0 else TG * (n - 1))
                        hp = e % 2
                        nc.scalar.copy(h_hi[hp][:], h[:]).then_inc(hhi_done, 1)
                        if e == 1:
                            eng.wait_ge(wt_done, 2 * g + 1)
                            nc.scalar.copy(wexp[0:E, :], D[0][0:E, :]).then_inc(wx_done, 1)
                            eng.wait_ge(wt_done, 2 * g + 2)
                            nc.scalar.copy(wexp[:], D[1][:]).then_inc(wx_done, 1)
                        if e < E and not (last and e >= E - 2):
                            eng.wait_ge(u_ready, n + 1)
                            high_gu(E * g + e + 2, e % 2)
                        if e < E and not (last and e >= E - 1):
                            if not (isinstance(g, int) and g == 0 and e == 0):
                                eng.wait_ge(d_ready, TG * n)
                            high_dn(E * g + e + 1, (e + 1) % 2)
                    if not last:
                        for t in range(TG):
                            tile_root(TG * g + TG + t)
                            if t:
                                tile_high(t - 1, TG * g + TG + t - 1)
                        tile_high(TG - 1, TG * g + 2 * TG - 1)

                steps(0)
                with eng.Fori(1, NG - 1) as g:
                    steps(g)
                steps(NG - 1, last=True)

            @block.vector
            def _(eng):
                def tile_low(t, T):
                    eng.wait_ge(xhi_done, T + 1)
                    cols = slice(t * P, (t + 1) * P)
                    nc.vector.tensor_tensor(xlo[:, :, cols], tile_ps[t % 2][:].rearrange("p (c n) -> p c n", c=NC),
                                            xhi[:, :, cols].bitcast(F32), ALU.subtract).then_inc(xlo_done, 1)

                def sweep(k, accumulate=None):
                    for t in range(TG):
                        T = TG * k + t
                        eng.wait_ge(xs_in[t % 2], 64 * k + 16 * (t // 2 + 1))
                        if not (isinstance(T, int) and T < 1):
                            eng.wait_ge(xs_done, T)
                        nc.vector.bn_stats(st[:, 0, :], xs[t % 2][:, 0:HALF])
                        nc.vector.bn_stats(st[:, 1, :], xs[t % 2][:, HALF:L]).then_inc(st_done, 1)
                        eng.wait_ge(st_done, 3 * T + 1)
                        if accumulate:
                            accumulate(t)
                        nc.vector.bn_aggr(mv[:], st[:].rearrange("p a b -> p (a b)")).then_inc(st_done, 1)
                        if t:
                            tile_low(t - 1, T - 1)
                        eng.wait_ge(sd_done, T + 1)
                        nc.vector.reciprocal(rs[:], sd[:]).then_inc(st_done, 1)
                        eng.wait_ge(st_done, 3 * T + 3)
                        nc.vector.tensor_scalar(xs[t % 2][:], xs[t % 2][:], mv[:, 0:1], rs[:, 0:1], ALU.subtract,
                                                ALU.mult).then_inc(xs_done, 1)
                    tile_low(TG - 1, TG * k + TG - 1)

                def route(g):
                    n = [0]

                    def link(ins):
                        n[0] += 1
                        ins.then_inc(rt, 1)
                        eng.wait_ge(rt, RTS * g + n[0])

                    lg = U[:, 0:TG * E].rearrange("p (t e) -> p t e", t=TG)
                    row = col[:].rearrange("p (t o) -> p t o", o=1).to_broadcast([P, TG, E])
                    eng.wait_ge(lg_done, g + 1)
                    link(nc.vector.tensor_reduce(col[:], lg, AX.X, ALU.max))
                    link(nc.vector.tensor_tensor(sc[:], lg, row, ALU.subtract))
                    eng.wait_ge(ex_done, g + 1)
                    link(nc.vector.tensor_reduce(col[:], sc[:], AX.X, ALU.add))
                    link(nc.vector.reciprocal(col[:], col[:]))
                    link(nc.vector.tensor_tensor(sc[:], sc[:], row, ALU.mult))
                    left = sc
                    for c in range(2):
                        link(nc.vector.tensor_reduce(col[:], left[:], AX.X, ALU.max))
                        link(nc.vector.tensor_tensor(oh[:], left[:], row, ALU.is_equal))
                        link(nc.vector.tensor_tensor(oh[:], oh[:], order[:], ALU.mult))
                        link(nc.vector.tensor_reduce(col[:], oh[:], AX.X, ALU.max))
                        if c == 0:
                            link(nc.vector.tensor_tensor(w[:], oh[:], row, ALU.is_equal))
                            link(nc.vector.scalar_tensor_tensor(out=ta[:], in0=w[:], scalar=-2.0, in1=sc[:],
                                                                op0=ALU.mult, op1=ALU.add))
                            left = ta
                        else:
                            link(nc.vector.tensor_tensor(oh[:], oh[:], row, ALU.is_equal))
                            link(nc.vector.tensor_tensor(w[:], w[:], oh[:], ALU.add))
                    link(nc.vector.scalar_tensor_tensor(out=w[:], in0=w[:], scalar=gt[:, 0:1], in1=sc[:],
                                                        op0=ALU.mult, op1=ALU.mult))
                    assert n[0] == RTS, n[0]

                def acc(g, e, t):
                    q = TG * (NS * g + e) + t
                    eng.wait_ge(d_ready, q + 1)
                    if e == 0:
                        if t == 0:
                            eng.wait_ge(y_in, 128 * g + 128)
                    else:
                        eng.wait_ge(acc_done, q - TG + 1)
                    if e < E:
                        nc.vector.scalar_tensor_tensor(out=y[:, t, :], in0=D[t % 2][:], scalar=w[:, t, e:e + 1],
                                                       in1=y[:, t, :], op0=ALU.mult, op1=ALU.add).then_inc(acc_done, 1)
                    else:
                        nc.vector.tensor_tensor(y[:, t, :], D[t % 2][:], y[:, t, :], ALU.add).then_inc(acc_done, 1)

                def steps(g, last=False):
                    route(g)
                    for e in range(NS):
                        n = NS * g + e
                        if e < E:
                            eng.wait_ge(u_ready, n + 1)
                            eng.wait_ge(silu_done, E * g + e + 1)
                            nc.vector.tensor_tensor(h[:], U[:], h[:], ALU.mult).then_inc(h_done, 1)
                        else:
                            eng.wait_ge(u_ready, n + 1)
                            eng.wait_ge(wx_done, 2 * g + 2)
                            eng.wait_ge(hlo_done, n)
                            nc.vector.tensor_tensor(h[:], G[:], wexp[:], ALU.mult).then_inc(h_done, 1)
                        if e:
                            acc(g, e - 1, 0)
                            acc(g, e - 1, 1)
                        eng.wait_ge(hhi_done, n + 1)
                        nc.vector.tensor_tensor(h_lo[e % 2][:], h[:], h_hi[e % 2][:].bitcast(F32),
                                                ALU.subtract).then_inc(hlo_done, 1)
                        if e:
                            for t in range(2, TG):
                                acc(g, e - 1, t)
                    if last:
                        for t in range(TG):
                            acc(g, E, t)
                    else:
                        sweep(g + 1, lambda t: acc(g, E, t))

                nc.vector.memset(epsc[:], EPS).then_inc(misc, 1)
                eng.wait_ge(misc, 3)
                nc.vector.tensor_tensor(rg_lo[:], rg[:], rg_hi[:].bitcast(F32), ALU.subtract).then_inc(misc, 1)
                sweep(0)
                steps(0)
                with eng.Fori(1, NG - 1) as g:
                    steps(g)
                steps(NG - 1, last=True)

            @block.tensor
            def _(eng):
                def split3(out, a, b, start, stop):
                    nc.tensor.matmul(out, a[0], b[0], start=start, stop=False)
                    nc.tensor.matmul(out, a[0], b[1], start=False, stop=False)
                    return nc.tensor.matmul(out, a[1], b[0], start=False, stop=stop)

                def first(g, e):
                    n = NS * g + e
                    if not (isinstance(g, int) and g == 0 and e == 0):
                        eng.wait_ge(h_done, n)
                    if e == 0:
                        eng.wait_ge(xlo_done, TG * g + TG)
                    if e < E:
                        eng.wait_ge(gulo_done, E * g + e + 1)
                    else:
                        eng.wait_ge(lora_split, 4)
                    for k, out in enumerate((G, U) if e < E else (G,)):
                        if k == 1 and e == 0:
                            eng.wait_ge(rt, RTS * g + 2)
                        for half in range(TOK // HALF):
                            cols = slice(half * HALF, (half + 1) * HALF)
                            for c in range(NC):
                                if e < E:
                                    a = gu_hi[e % 2][:, k, c, :], gu_lo[e % 2][:, k, c, :]
                                else:
                                    a = la_hi[:, c, :], la_lo[:, c, :]
                                mm = split3(out[:, cols], a, (xhi[:, c, cols], xlo[:, c, cols]), c == 0, c == NC - 1)
                        if e < E:
                            mm.then_inc(g_ready if k == 0 else u_ready, 1)
                        else:
                            mm.then_inc(u_ready, 1)

                def second(g, e, t):
                    n = NS * g + e
                    q = TG * n + t
                    if t == 0:
                        eng.wait_ge(hlo_done, n + 1)
                        if e < E:
                            eng.wait_ge(dnlo_done, E * g + e + 1)
                    if not (isinstance(g, int) and g == 0 and e == 0 and t < 2):
                        eng.wait_ge(acc_done, q - 1)
                    if e == 0 and t < 2:
                        eng.wait_ge(wx_done, 2 * g + t + 1)
                    a = h_hi[e % 2][:, t * P:(t + 1) * P], h_lo[e % 2][:, t * P:(t + 1) * P]
                    bh, bl = (dn_hi[e % 2], dn_lo[e % 2]) if e < E else (lb_hi, lb_lo)
                    for half in range(L // HALF):
                        cols = slice(half * HALF, (half + 1) * HALF)
                        mm = split3(D[t % 2][:, cols], a, (bh[:, cols], bl[:, cols]), True, True)
                    mm.then_inc(d_ready, 1)

                def transposes(t, T):
                    eng.wait_ge(xs_done, T + 1)
                    if not (isinstance(T, int) and T < 2):
                        if t >= 2:
                            eng.wait_ge(xlo_done, T - 1)
                    for c in range(NC):
                        mm = nc.tensor.transpose(tile_ps[t % 2][:, c * P:(c + 1) * P], xs[t % 2][:, c * P:(c + 1) * P],
                                                 ident[:])
                    mm.then_inc(tr_done, 1)

                def logits(k):
                    eng.wait_ge(xlo_done, TG * k + TG)
                    for t in range(TG):
                        cols = slice(t * P, (t + 1) * P)
                        for c in range(NC):
                            mm = split3(U[:, t * E:(t + 1) * E], (xhi[:, c, cols], xlo[:, c, cols]),
                                        (rg_hi[:, c, :], rg_lo[:, c, :]), c == 0, c == NC - 1)
                    mm.then_inc(lg_done, 1)

                def spread(g):
                    eng.wait_ge(rt, RTS * (g + 1))
                    if not (isinstance(g, int) and g == 0):
                        eng.wait_ge(acc_done, TG * NS * g)
                    for t in range(TG):
                        mm = nc.tensor.transpose(D[0][0:E, t * P:(t + 1) * P], w[:, t, :], ident[:])
                    mm.then_inc(wt_done, 1)
                    eng.wait_ge(wx_done, 2 * g + 1)
                    for half in range(TOK // HALF):
                        cols = slice(half * HALF, (half + 1) * HALF)
                        mm = nc.tensor.matmul(D[1][:, cols], sel[:], wexp[0:E, cols], start=True, stop=True)
                    mm.then_inc(wt_done, 1)

                def steps(g, last=False):
                    first(g, 0)
                    for e in range(1, NS):
                        first(g, e)
                        if e == 1:
                            spread(g)
                        for t in range(TG):
                            second(g, e - 1, t)
                    for t in range(TG):
                        second(g, E, t)
                        if not last and t:
                            transposes(t - 1, TG * g + TG + t - 1)
                    if not last:
                        transposes(TG - 1, TG * g + 2 * TG - 1)
                        logits(g + 1)

                eng.wait_ge(const_in, 80)
                eng.wait_ge(misc, 4)
                for t in range(TG):
                    transposes(t, t)
                logits(0)
                steps(0)
                with eng.Fori(1, NG - 1) as g:
                    steps(g)
                steps(NG - 1, last=True)


def build(nc, x, c, k, dskip, g1, g2, ident, gu, dn, la, lb, rg, order, sel, out):
    kpad = nc.dram_tensor("kpad", [NH, KW], F32).ap()
    x1 = nc.dram_tensor("x1", [NT, P, L], F32).ap()
    stage1(nc, x, c, k, dskip, g1, ident, kpad, x1)
    stage2(nc, x1, gu, dn, la, lb, rg, g2, ident, order, sel, out)


def kernel(**inputs):
    import numpy as np
    import concourse.bacc as bacc
    from concourse.bass_utils import run_bass_kernel_spmd
    a = {n: np.asarray(v) for n, v in inputs.items()}

    def rows(t):
        return np.ascontiguousarray(t.reshape(B, NT, CT, L).transpose(1, 2, 0, 3)).reshape(NT, P, L)

    def model_major(t):
        return t.reshape(t.shape[0], t.shape[1], NC, P).transpose(0, 3, 2, 1)

    c = a["ctx_2048"].reshape(B, NT, HT, HD, NC, P).transpose(1, 5, 2, 4, 3, 0)[:, ::-1].reshape(NT, P, HT, NC, IB)
    k = a["L0_xattn_ssm_kernel"]
    arrays = {
        "x": rows(a["x"]),
        "c": np.ascontiguousarray(np.concatenate([c, c[..., :IB // 2]], axis=-1)),
        "k": np.ascontiguousarray(np.pad(k, ((0, 0), (P - 1, 1)))),
        "dskip": np.ascontiguousarray(a["L0_xattn_D"].reshape(NH, 1)),
        "g1": np.ascontiguousarray(np.broadcast_to(a["g_xattn"].reshape(1, 1), (P, 1))),
        "g2": np.ascontiguousarray(np.broadcast_to(a["g_ffn"].reshape(1, 1), (P, 1))),
        "ident": np.eye(P, dtype=np.float32),
        "gu": np.ascontiguousarray(np.stack([model_major(a["L0_ffn_gate_w"]), model_major(a["L0_ffn_up_w"])], axis=2)),
        "dn": np.ascontiguousarray(a["L0_ffn_down_w"].transpose(0, 2, 1)),
        "la": np.ascontiguousarray(model_major(a["L0_ffn_lora_A"].reshape(1, E * R, L))[0]),
        "lb": np.ascontiguousarray(a["L0_ffn_lora_B"].transpose(0, 2, 1).reshape(E * R, L)),
        "rg": np.ascontiguousarray(a["L0_ffn_G"].reshape(NC, P, E).transpose(1, 0, 2)),
        "order": np.ascontiguousarray(np.broadcast_to(np.arange(E, 0, -1, dtype=np.float32), (P, TG, E))),
        "sel": np.repeat(np.eye(E, dtype=np.float32), R, axis=1),
    }
    nc = bacc.Bacc("TRN2", target_bir_lowering=False, num_devices=1)
    ins = [nc.dram_tensor("in_" + n, v.shape, mybir.dt.from_np(v.dtype), kind="ExternalInput").ap() for n, v in arrays.items()]
    out = nc.dram_tensor("out", (NT, P, L), F32, kind="ExternalOutput").ap()
    build(nc, *ins, out)
    r = run_bass_kernel_spmd(nc, [{"in_" + n: v for n, v in arrays.items()}], core_ids=[0])
    y = r.results[0]["out"]
    return np.ascontiguousarray(y.reshape(NT, CT, B, L).transpose(2, 0, 1, 3)).reshape(B, CH, L)
```

```python
from contextlib import ExitStack

import concourse.bass as bass
from concourse import mybir

F32 = mybir.dt.float32
F32R = mybir.dt.float32r
ALU = mybir.AluOpType
ACT = mybir.ActivationFunctionType
AX = mybir.AxisListType

P = 128
B, CH, L = 8, 512, 1024
HD = 8
NH = CH // HD
HT = 2
CT = HT * HD
NT = CH // CT
NC = L // P
IB = HD * B
WR = IB + IB // 2
ND = 4
YC = ND * IB + IB // 2
FULL = ND * IB
SK = IB + B
ZS = 9
ZC = ZS * IB
ZB = 5 * IB
ZE = 8 * IB
KW = L + P
NP = NC // 2
EPS = 1e-5

E, F, R = 8, 128, 16
TG = 8
NG = NT // TG
TOK = TG * P
HALF = 512
NS = E + 1


def view(ap, dims, shift=0):
    return bass.AP(tensor=ap.tensor, offset=ap.offset + shift, ap=[list(ap.ap[0])] + [list(d) for d in dims])


def stage1(nc, x_d, c_d, k_d, dskip_d, g_d, ident_d, kpad_d, x1_d):
    ctx = ExitStack()
    with ctx:
        sb = lambda n, s, dt=F32: ctx.enter_context(nc.sbuf_tensor(n, s, dt))
        sem = lambda n: ctx.enter_context(nc.semaphore(n))
        x_nat = [sb(f"x_nat{p}", [P, L]) for p in range(2)]
        x_new = [sb(f"x_new{p}", [P, L]) for p in range(2)]
        xn = sb("xn", [P, L])
        cT = [sb(f"cT{p}", [P, HT, NC, WR]) for p in range(2)]
        qT = [sb(f"qT{p}", [P, HT, NC, WR]) for p in range(2)]
        kv = [sb(f"kv{h}", [P, NC, YC]) for h in range(HT)]
        kvhi = [sb(f"kvhi{h}", [P, NC, YC], F32R) for h in range(HT)]
        kvlo = [sb(f"kvlo{h}", [P, NC, YC], F32R) for h in range(HT)]
        t_raw = [sb(f"t_raw{h}", [P, L]) for h in range(HT)]
        t_hi = [sb(f"t_hi{h}", [P, L], F32R) for h in range(HT)]
        t_lo = [sb(f"t_lo{h}", [P, L], F32R) for h in range(HT)]
        oT = [sb(f"oT{p}", [P, NC, P]) for p in range(2)]
        z = [sb(f"z{p}", [P, 2, ZC]) for p in range(2)]
        ident = sb("ident", [P, P])
        krow = sb("krow", [NH, KW])
        dcol = sb("dcol", [NH, 1])
        gate = sb("gate", [P, 1])
        gt = sb("gt", [P, 1])
        epsc = sb("epsc", [P, 1])
        st = sb("st", [P, 2, 6])
        mv = sb("mv", [P, 2])
        sd = sb("sd", [P, 1])
        rs = sb("rs", [P, 1])
        Y = [ctx.enter_context(nc.psum_tensor(f"Y{s}", [P, 2, HALF], F32)) for s in range(2)]
        OP = ctx.enter_context(nc.psum_tensor("OP", [P, L], F32))
        XP = ctx.enter_context(nc.psum_tensor("XP", [P, L], F32))

        const_in = sem("const_in")
        k_in = sem("k_in")
        k_sum = sem("k_sum")
        k_out = sem("k_out")
        gate_ready = sem("gate_ready")
        x_in = [sem(f"x_in{p}") for p in range(2)]
        c_in = [sem(f"c_in{p}") for p in range(2)]
        t_in = [sem(f"t_in{h}") for h in range(HT)]
        thi_done = sem("thi_done")
        tlo_done = sem("tlo_done")
        kv_done = sem("kv_done")
        kvhi_done = sem("kvhi_done")
        kvlo_done = [sem(f"kvlo_done{h}") for h in range(HT)]
        y_ready = sem("y_ready")
        z_done = sem("z_done")
        z_zero = sem("z_zero")
        sum_done = sem("sum_done")
        o_ready = sem("o_ready")
        res_done = sem("res_done")
        x_out = [sem(f"x_out{p}") for p in range(2)]
        st_done = sem("st_done")
        sd_done = sem("sd_done")
        xn_done = sem("xn_done")
        xt_ready = sem("xt_ready")
        q_done = sem("q_done")

        def kernel_window(n):
            return bass.AP(tensor=kpad_d.tensor, offset=n * KW, ap=[[1, P], [1, L]])

        with nc.Block() as block:

            @block.sync
            def _(eng):
                eng.dma_start(krow[:], k_d).then_inc(k_in, 16)
                eng.dma_start(dcol[:], dskip_d).then_inc(k_in, 16)
                eng.dma_start(x_nat[0][:], x_d[0]).then_inc(x_in[0], 16)
                eng.dma_start(cT[0][:], c_d[0]).then_inc(c_in[0], 16)
                eng.dma_start(ident[:], ident_d).then_inc(const_in, 16)
                eng.dma_start(gate[:], g_d).then_inc(const_in, 16)
                eng.wait_ge(k_sum, 1)
                eng.dma_start(kpad_d, krow[:]).then_inc(k_out, 16)
                eng.dma_start(cT[1][:], c_d[1]).then_inc(c_in[1], 16)
                eng.wait_ge(k_out, 16)
                for h in range(HT):
                    eng.dma_start(t_raw[h][:], kernel_window(h)).then_inc(t_in[h], 16)

                def body(i, p, first=False, last=False):
                    if not last:
                        for h in range(HT):
                            eng.wait_ge(thi_done, 2 * i + h + 1)
                            eng.wait_ge(tlo_done, 2 * i + h + 1)
                            eng.dma_start(t_raw[h][:], kernel_window(2 * i + 2 + h)).then_inc(t_in[h], 16)
                    if not first:
                        eng.wait_ge(res_done, i)
                    if not last:
                        eng.dma_start(x_nat[1 - p][:], x_d[i + 1]).then_inc(x_in[1 - p], 16)
                    if not first:
                        eng.dma_start(x1_d[i - 1], x_new[1 - p][:]).then_inc(x_out[1 - p], 16)
                        if not last:
                            eng.wait_ge(kv_done, 4 * i)
                            eng.dma_start(cT[1 - p][:], c_d[i + 1]).then_inc(c_in[1 - p], 16)

                body(0, 0, first=True)
                body(1, 1)
                with eng.Fori(1, NT // 2 - 1) as k:
                    for p in range(2):
                        body(2 * k + p, p)
                body(NT - 2, 0)
                body(NT - 1, 1, last=True)
                eng.wait_ge(res_done, NT)
                eng.dma_start(x1_d[NT - 1], x_new[1][:]).then_inc(x_out[1], 16)
                for p in range(2):
                    eng.wait_ge(x_out[p], 16 * (NT // 2))

            @block.gpsimd
            def _(eng):
                def products(n, h, half, p, have):
                    eng.wait_ge(c_in[p], have)
                    if not (isinstance(n, int) and n < HT):
                        eng.wait_ge(kvhi_done, 2 * (n - HT) + half + 1)
                        eng.wait_ge(kvlo_done[h], (n - HT - h) + half + 1)
                    c0 = half * (NC // 2)
                    cc = cT[p][:, h, c0:c0 + NC // 2, 0:IB]
                    o = kv[h][:, c0:c0 + NC // 2, 0:IB]
                    nc.gpsimd.tensor_tensor(view(o, [[YC, NC // 2], [IB, ND], [1, IB]]),
                                            view(cc, [[WR, NC // 2], [0, ND], [1, IB]]),
                                            view(cc, [[WR, NC // 2], [B, ND], [1, IB]]), ALU.mult)
                    nc.gpsimd.tensor_tensor(kv[h][:, c0:c0 + NC // 2, FULL:YC],
                                            cT[p][:, h, c0:c0 + NC // 2, 0:IB // 2],
                                            cT[p][:, h, c0:c0 + NC // 2, IB // 2:IB], ALU.mult).then_inc(kv_done, 1)

                def low(n, h):
                    eng.wait_ge(thi_done, n + 1)
                    nc.gpsimd.tensor_tensor(t_lo[h][:], t_raw[h][:], t_hi[h][:].bitcast(F32),
                                            ALU.subtract).then_inc(tlo_done, 1)
                    if h == 1:
                        for half in range(2):
                            eng.wait_ge(kvhi_done, 2 * n + half + 1)
                            c0 = half * (NC // 2)
                            nc.gpsimd.tensor_tensor(kvlo[h][:, c0:c0 + NC // 2, :], kv[h][:, c0:c0 + NC // 2, :],
                                                    kvhi[h][:, c0:c0 + NC // 2, :].bitcast(F32),
                                                    ALU.subtract).then_inc(kvlo_done[h], 1)

                for n in range(HT):
                    products(n, n, 0, 0, 16)
                    products(n, n, 1, 0, 16)
                low(0, 0)

                def body(i, p, k, last=False):
                    low(2 * i + 1, 1)
                    if not last:
                        products(2 * i + 2, 0, 0, 1 - p, 16 * (k + 1 + p))
                        products(2 * i + 2, 0, 1, 1 - p, 16 * (k + 1 + p))
                        low(2 * i + 2, 0)
                        products(2 * i + 3, 1, 0, 1 - p, 16 * (k + 1 + p))
                        products(2 * i + 3, 1, 1, 1 - p, 16 * (k + 1 + p))

                body(0, 0, 0)
                body(1, 1, 0)
                with eng.Fori(1, NT // 2 - 1) as k:
                    for p in range(2):
                        body(2 * k + p, p, k)
                body(NT - 2, 0, NT // 2 - 1)
                body(NT - 1, 1, NT // 2 - 1, last=True)

            @block.scalar
            def _(eng):
                def high_t(n, h, have):
                    eng.wait_ge(t_in[h], have)
                    if not (isinstance(n, int) and n < HT):
                        eng.wait_ge(y_ready, NP * (n - 1))
                    nc.scalar.copy(t_hi[h][:], t_raw[h][:]).then_inc(thi_done, 1)

                def high_kv(n, h):
                    for half in range(2):
                        eng.wait_ge(kv_done, 2 * n + half + 1)
                        if half == 0 and not (isinstance(n, int) and n < HT):
                            eng.wait_ge(y_ready, NP * (n - 1))
                        c0 = half * (NC // 2)
                        nc.scalar.copy(kvhi[h][:, c0:c0 + NC // 2, :],
                                       kv[h][:, c0:c0 + NC // 2, :]).then_inc(kvhi_done, 1)

                def root(i):
                    eng.wait_ge(st_done, 3 * i + 2)
                    nc.scalar.activation(sd[:], mv[:, 1:2], ACT.Sqrt, bias=epsc[:, 0:1]).then_inc(sd_done, 1)

                def take_q(i, p):
                    eng.wait_ge(xt_ready, i + 1)
                    if not (isinstance(i, int) and i < 2):
                        eng.wait_ge(z_done, 8 * (i - 1))
                    src = XP[:]
                    nc.scalar.copy(qT[p][:, :, :, 0:IB], view(src, [[IB, HT], [P, NC], [1, IB]]))
                    nc.scalar.copy(qT[p][:, :, :, IB:WR], view(src, [[IB, HT], [P, NC], [1, IB // 2]])) \
                        .then_inc(q_done, 1)

                eng.wait_ge(const_in, 32)
                nc.scalar.activation(gt[:], gate[:], ACT.Tanh).then_inc(gate_ready, 1)
                root(0)
                high_t(0, 0, 16)
                high_kv(0, 0)
                take_q(0, 0)

                def body(i, p, k, last=False):
                    high_t(2 * i + 1, 1, 16 * (i + 1))
                    high_kv(2 * i + 1, 1)
                    if not last:
                        root(i + 1)
                        high_t(2 * i + 2, 0, 16 * (i + 2))
                        high_kv(2 * i + 2, 0)
                        take_q(i + 1, 1 - p)

                body(0, 0, 0)
                body(1, 1, 0)
                with eng.Fori(1, NT // 2 - 1) as k:
                    for p in range(2):
                        body(2 * k + p, p, k)
                body(NT - 2, 0, NT // 2 - 1)
                body(NT - 1, 1, NT // 2 - 1, last=True)

            @block.vector
            def _(eng):
                def multiply(i, p, h, r):
                    s = r % 2
                    idx = 8 * i + 4 * h + r
                    eng.wait_ge(y_ready, idx + 1)
                    if h == 0 and r == 0:
                        eng.wait_ge(q_done, i + 1)
                    if not (isinstance(i, int) and i == 0 and h == 0 and r < 2):
                        eng.wait_ge(sum_done, idx - 1)
                    y = Y[s][:, :, 0:YC]
                    q = qT[p][:, h, 2 * r:2 * r + 2, :]
                    zz = z[s][:]
                    nc.vector.tensor_tensor(view(zz, [[ZC, 2], [SK, ND], [1, IB]]),
                                            view(y, [[HALF, 2], [IB, ND], [1, IB]]),
                                            view(q, [[WR, 2], [0, ND], [1, IB]]), ALU.mult)
                    nc.vector.tensor_tensor(view(zz, [[ZC, 2], [IB, ND - 1], [1, IB]], ZB),
                                            view(y, [[HALF, 2], [IB, ND - 1], [1, IB]], IB),
                                            view(q, [[WR, 2], [B, ND - 1], [1, IB]], B), ALU.mult)
                    nc.vector.tensor_tensor(view(zz, [[ZC, 2], [IB // 2, 2], [1, IB // 2]], ZE),
                                            view(y, [[HALF, 2], [0, 2], [1, IB // 2]], FULL),
                                            view(q, [[WR, 2], [IB // 2, 2], [1, IB // 2]], IB // 2),
                                            ALU.mult).then_inc(z_done, 1)

                def total(i, p, h, r):
                    s = r % 2
                    eng.wait_ge(z_done, 8 * i + 4 * h + r + 1)
                    if h == 0 and r == 0 and not (isinstance(i, int) and i < 2):
                        eng.wait_ge(o_ready, i - 1)
                    nc.vector.tensor_reduce(oT[p][:, 2 * r:2 * r + 2, h * IB:(h + 1) * IB],
                                            view(z[s][:], [[ZC, 2], [1, IB], [IB, ZS]]), AX.X,
                                            ALU.add).then_inc(sum_done, 1)

                def low_kv(n, h, half):
                    eng.wait_ge(kvhi_done, 2 * n + half + 1)
                    c0 = half * (NC // 2)
                    nc.vector.tensor_tensor(kvlo[h][:, c0:c0 + NC // 2, :], kv[h][:, c0:c0 + NC // 2, :],
                                            kvhi[h][:, c0:c0 + NC // 2, :].bitcast(F32),
                                            ALU.subtract).then_inc(kvlo_done[h], 1)

                def stats(i, p, have):
                    eng.wait_ge(x_in[p], have)
                    if not (isinstance(i, int) and i < 1):
                        eng.wait_ge(xn_done, i)
                    nc.vector.bn_stats(st[:, 0, :], x_nat[p][:, 0:HALF])
                    nc.vector.bn_stats(st[:, 1, :], x_nat[p][:, HALF:L]).then_inc(st_done, 1)

                def aggregate(i):
                    nc.vector.bn_aggr(mv[:], st[:].rearrange("p a b -> p (a b)")).then_inc(st_done, 1)

                def invert(i):
                    eng.wait_ge(sd_done, i + 1)
                    nc.vector.reciprocal(rs[:], sd[:]).then_inc(st_done, 1)

                def normalize(i, p):
                    eng.wait_ge(st_done, 3 * i + 3)
                    if not (isinstance(i, int) and i < 1):
                        eng.wait_ge(xt_ready, i)
                    nc.vector.tensor_scalar(xn[:], x_nat[p][:], mv[:, 0:1], rs[:, 0:1], ALU.subtract,
                                            ALU.mult).then_inc(xn_done, 1)

                def residual(i, p):
                    eng.wait_ge(o_ready, i + 1)
                    if not (isinstance(i, int) and i < 2):
                        eng.wait_ge(x_out[p], stored[p](i))
                    nc.vector.scalar_tensor_tensor(out=x_new[p][:], in0=OP[:], scalar=gt[:, 0:1],
                                                   in1=x_nat[p][:], op0=ALU.mult,
                                                   op1=ALU.add).then_inc(res_done, 1)

                stored = [lambda i: 8 * i, lambda i: 8 * i - 8]

                nc.vector.memset(epsc[:], EPS)
                nc.vector.memset(z[0][:], 0.0)
                nc.vector.memset(z[1][:], 0.0).then_inc(z_zero, 1)
                eng.wait_ge(k_in, 32)
                nc.vector.tensor_tensor(krow[:, P - 1:P], krow[:, P - 1:P], dcol[:], ALU.add).then_inc(k_sum, 1)
                eng.wait_ge(z_zero, 1)
                stats(0, 0, 16)
                eng.wait_ge(st_done, 1)
                aggregate(0)
                invert(0)
                normalize(0, 0)
                low_kv(0, 0, 0)
                low_kv(0, 0, 1)
                eng.wait_ge(gate_ready, 1)

                def body(i, p, k, first=False, last=False):
                    multiply(i, p, 0, 0)
                    if not first:
                        total(i - 1, 1 - p, 1, 3)
                    multiply(i, p, 0, 1)
                    total(i, p, 0, 0)
                    multiply(i, p, 0, 2)
                    total(i, p, 0, 1)
                    if not first:
                        residual(i - 1, 1 - p)
                    multiply(i, p, 0, 3)
                    total(i, p, 0, 2)
                    if not last:
                        stats(i + 1, 1 - p, 16 * (k + 1 + p))
                    multiply(i, p, 1, 0)
                    if not last:
                        eng.wait_ge(st_done, 3 * i + 4)
                    total(i, p, 0, 3)
                    if not last:
                        aggregate(i + 1)
                    multiply(i, p, 1, 1)
                    if not last:
                        invert(i + 1)
                    total(i, p, 1, 0)
                    if not last:
                        normalize(i + 1, 1 - p)
                    if not last:
                        low_kv(2 * i + 2, 0, 0)
                    multiply(i, p, 1, 2)
                    total(i, p, 1, 1)
                    if not last:
                        low_kv(2 * i + 2, 0, 1)
                    multiply(i, p, 1, 3)
                    total(i, p, 1, 2)

                body(0, 0, 0, first=True)
                body(1, 1, 0)
                with eng.Fori(1, NT // 2 - 1) as k:
                    for p in range(2):
                        body(2 * k + p, p, k)
                body(NT - 2, 0, NT // 2 - 1)
                body(NT - 1, 1, NT // 2 - 1, last=True)
                total(NT - 1, 1, 1, 3)
                residual(NT - 1, 1)

            @block.tensor
            def _(eng):
                def conv(i, h, r):
                    n = 2 * i + h
                    idx = 8 * i + 4 * h + r
                    s2 = r % 2
                    if r == 0:
                        eng.wait_ge(tlo_done, n + 1)
                        eng.wait_ge(kvlo_done[h], 2 * i + 1)
                    if r == 2:
                        eng.wait_ge(kvlo_done[h], 2 * i + 2)
                    if not (isinstance(i, int) and i == 0 and h == 0 and r < 2):
                        eng.wait_ge(z_done, idx - 1)
                    for a in range(2):
                        c = 2 * r + a
                        for s in range(c + 1):
                            w = slice((c - s) * P, (c - s + 1) * P)
                            for t, m in ((t_hi, kvhi), (t_hi, kvlo), (t_lo, kvhi)):
                                mm = nc.tensor.matmul(Y[s2][:, a, 0:YC], t[h][:, w], m[h][:, s, :],
                                                      start=(s == 0 and t is t_hi and m is kvhi),
                                                      stop=(s == c and t is t_lo))
                    mm.then_inc(y_ready, 1)

                def transpose_x(i):
                    eng.wait_ge(xn_done, i + 1)
                    if not (isinstance(i, int) and i < 1):
                        eng.wait_ge(q_done, i)
                    for c in range(NC):
                        mm = nc.tensor.transpose(XP[:, c * P:(c + 1) * P], xn[:, c * P:(c + 1) * P], ident[:])
                    mm.then_inc(xt_ready, 1)

                def transpose_o(i, p):
                    eng.wait_ge(sum_done, 8 * i + 8)
                    if not (isinstance(i, int) and i < 1):
                        eng.wait_ge(res_done, i)
                    for c in range(NC):
                        mm = nc.tensor.transpose(OP[:, c * P:(c + 1) * P], oT[p][:, c, :], ident[:])
                    mm.then_inc(o_ready, 1)

                eng.wait_ge(const_in, 32)
                transpose_x(0)

                def body(i, p, first=False, last=False):
                    for r in range(NP):
                        conv(i, 0, r)
                        if r == 2 and not first:
                            transpose_o(i - 1, 1 - p)
                    for r in range(NP):
                        conv(i, 1, r)
                        if r == 2 and not last:
                            transpose_x(i + 1)

                body(0, 0, first=True)
                body(1, 1)
                with eng.Fori(1, NT // 2 - 1) as k:
                    for p in range(2):
                        body(2 * k + p, p)
                body(NT - 2, 0)
                body(NT - 1, 1, last=True)
                transpose_o(NT - 1, 1)


E, F, R = 8, 128, 16
ER = E * R
TG = 8
NG = NT // TG
HALF = 512
TOKENS = NT * P
RC = TOKENS + P
SPARE = E * RC
SLOTS = 2 * TOKENS // P + E
ROWS = SPARE + P
MADE = SLOTS * P
RTS = 28


class Chosen:

    def __init__(self, nc, ctx):
        sb = lambda n, s, dt=F32: ctx.enter_context(nc.sbuf_tensor(n, s, dt))
        self.lt_hi = sb("lt_hi", [P, TOKENS], F32R)
        self.lt_lo = sb("lt_lo", [P, TOKENS], F32R)
        self.row = sb("row", [P, 2, NT], mybir.dt.uint32)
        self.w = sb("wsel", [P, 2, NT])
        self.table = sb("table", [P, 3, SLOTS], mybir.dt.int32)
        self.ends = sb("ends", [P, E], mybir.dt.int32)


def route_tokens(nc, ctx0, keep, x1_d, ag_d, g_d, ident_d, order_d, utri_d, ones_d, base_d, iota_d, grid_d, sorted_d):
    ctx = ExitStack()
    with ctx:
        sb = lambda n, s, dt=F32: ctx.enter_context(nc.sbuf_tensor(n, s, dt))
        sem = lambda n: ctx.enter_context(nc.semaphore(n))
        ps = lambda n, s: ctx.enter_context(nc.psum_tensor(n, s, F32))
        x_in_sb = [sb(f"xa{p}", [P, L]) for p in range(2)]
        xs = sb("xs", [P, TG, L])
        xt_hi = [sb(f"xt_hi{p}", [P, NC, P], F32R) for p in range(2)]
        xt_lo = [sb(f"xt_lo{p}", [P, NC, P], F32R) for p in range(2)]
        ag = sb("ag", [P, NC, ER + E])
        ag_hi = sb("ag_hi", [P, NC, ER + E], F32R)
        ag_lo = sb("ag_lo", [P, NC, ER + E], F32R)
        lr = sb("lr", [P, TG, ER + E])
        ident, utri, ones = sb("ident2", [P, P]), sb("utri", [P, P]), sb("ones", [P, P])
        zero = sb("zero", [P, L])
        order = sb("order", [P, TG, E])
        sc, ta, tb = sb("sc", [P, TG, E]), sb("ta", [P, TG, E]), sb("tb", [P, TG, E])
        oh = [sb(f"oh{c}", [P, TG, E]) for c in range(2)]
        col, top = sb("col", [P, TG]), [sb(f"top{c}", [P, TG]) for c in range(2)]
        place = sb("place", [P, 2, TG], mybir.dt.uint32)
        base = sb("base", [P, E])
        base0 = sb("base0", [P, E])
        iota = sb("iota", [P, 1])
        pad = sb("pad", [P, E], mybir.dt.uint32)
        grid = sb("grid", [P, SLOTS])
        nt, cum, low_ = sb("nt", [P, E]), sb("cum", [P, E + 1]), sb("low_", [P, E])
        nti = sb("nti", [P, E], mybir.dt.int32)
        big = [sb(f"big{c}", [P, SLOTS, E]) for c in range(3)]
        flat = [sb(f"flat{c}", [P, SLOTS]) for c in range(2)]
        gate, gt, epsc = sb("gate2", [P, 1]), sb("gt2", [P, 1]), sb("epsc2", [P, 1])
        st, mv, sd, rs = sb("st2", [P, 2, 6]), sb("mv2", [P, 2]), sb("sd2", [P, 1]), sb("rs2", [P, 1])
        XT = [ps(f"XT{p}", [P, L]) for p in range(2)]
        LR = [ps(f"LR{p}", [P, HALF]) for p in range(2)]
        LT = ps("LT", [P, L])

        const_in = sem("const_in2")
        xa_in = [sem(f"xa_in{p}") for p in range(2)]
        st_done = sem("st_done2")
        sd_done = sem("sd_done2")
        xs_done = sem("xs_done")
        tr_done = sem("tr_done")
        xhi_done, xlo_done = sem("xhi_done"), sem("xlo_done")
        ag_done = sem("ag_done")
        lr_done = sem("lr_done")
        rt = sem("rt")
        ex_done = sem("ex_done")
        pos_done = sem("pos_done")
        lt_done = sem("lt_done")
        lthi_done, ltlo_done = sem("lthi_done"), sem("ltlo_done")
        out_done = [sem(f"out_done{t}") for t in range(TG)]
        pad_done = sem("pad_done")
        misc = sem("misc")
        tab = sem("tab")

        with nc.Block() as block:

            @block.sync
            def _(eng):
                def load(t, T):
                    if not (isinstance(T, int) and T < 2):
                        eng.wait_ge(xs_done, T - 1)
                    eng.dma_start(x_in_sb[t % 2][:], x1_d[T]).then_inc(xa_in[t % 2], 16)

                load(0, 0)
                load(1, 1)
                for s, d in ((ident, ident_d), (gate, g_d), (order, order_d), (ag, ag_d), (utri, utri_d),
                             (ones, ones_d), (base0, base_d), (iota, iota_d), (grid, grid_d)):
                    eng.dma_start(s[:], d).then_inc(const_in, 16)
                for t in range(2, TG):
                    load(t, t)
                with eng.Fori(1, NG) as g:
                    for t in range(TG):
                        load(t, TG * g + t)

            @block.gpsimd
            def _(eng):
                def send(t, g):
                    for c in range(2):
                        eng.indirect_dma_start(out=sorted_d, out_offset=bass.IndirectOffsetOnAxis(ap=place[:, c, t:t + 1], axis=0),
                                               in_=xs[:, t, :], in_offset=None).then_inc(out_done[t], 16)

                for g in range(NG):
                    eng.wait_ge(rt, RTS * g + RTS)
                    for t in range(TG):
                        send(t, g)
                eng.wait_ge(tab, 1)
                for e in range(E):
                    eng.indirect_dma_start(out=sorted_d, out_offset=bass.IndirectOffsetOnAxis(ap=pad[:, e:e + 1], axis=0),
                                           in_=zero[:], in_offset=None).then_inc(pad_done, 16)
                eng.dma_start(sorted_d[SPARE:SPARE + P, :], zero[:]).then_inc(pad_done, 16)
                eng.wait_ge(pad_done, 16 * (E + 1))
                for t in range(TG):
                    eng.wait_ge(out_done[t], 32 * NG)

            @block.scalar
            def _(eng):
                eng.wait_ge(const_in, 144)
                nc.scalar.activation(gt[:], gate[:], ACT.Tanh).then_inc(misc, 1)
                nc.scalar.copy(ag_hi[:], ag[:]).then_inc(misc, 1)

                def high(t, T):
                    eng.wait_ge(tr_done, T + 1)
                    if not (isinstance(T, int) and T < 2):
                        eng.wait_ge(ag_done, T - 1)
                    nc.scalar.copy(xt_hi[t % 2][:], XT[t % 2][:].rearrange("p (c n) -> p c n", c=NC)).then_inc(xhi_done, 1)

                def take(t, T):
                    eng.wait_ge(ag_done, T + 1)
                    nc.scalar.copy(lr[:, t, :], LR[t % 2][:, 0:ER + E]).then_inc(lr_done, 1)

                def group(g):
                    for t in range(TG):
                        T = TG * g + t
                        if t:
                            high(t - 1, T - 1)
                        eng.wait_ge(st_done, 3 * T + 2)
                        nc.scalar.activation(sd[:], mv[:, 1:2], ACT.Sqrt, bias=epsc[:, 0:1]).then_inc(sd_done, 1)
                        if t > 1:
                            take(t - 2, T - 2)
                    high(TG - 1, TG * g + TG - 1)
                    take(TG - 2, TG * g + TG - 2)
                    take(TG - 1, TG * g + TG - 1)
                    eng.wait_ge(rt, RTS * g + 2)
                    nc.scalar.activation(sc[:], sc[:], ACT.Exp).then_inc(ex_done, 1)
                    eng.wait_ge(lt_done, g + 1)
                    nc.scalar.copy(keep.lt_hi[:, TG * P * g:TG * P * (g + 1)], LT[:]).then_inc(lthi_done, 1)

                for g in range(NG):
                    group(g)

            @block.vector
            def _(eng):
                def lows(t, T):
                    eng.wait_ge(xhi_done, T + 1)
                    nc.vector.tensor_tensor(xt_lo[t % 2][:], XT[t % 2][:].rearrange("p (c n) -> p c n", c=NC),
                                            xt_hi[t % 2][:].bitcast(F32), ALU.subtract).then_inc(xlo_done, 1)

                def sweep(g, first=False):
                    for t in range(TG):
                        T = TG * g + t
                        eng.wait_ge(xa_in[t % 2], (TG // 2 * 16) * g + 16 * (t // 2 + 1))
                        if not (first and t == 0):
                            eng.wait_ge(xs_done, T)
                        nc.vector.bn_stats(st[:, 0, :], x_in_sb[t % 2][:, 0:HALF])
                        nc.vector.bn_stats(st[:, 1, :], x_in_sb[t % 2][:, HALF:L]).then_inc(st_done, 1)
                        eng.wait_ge(st_done, 3 * T + 1)
                        if t:
                            lows(t - 1, T - 1)
                        else:
                            nc.vector.tensor_copy(sd[:], epsc[:])
                        nc.vector.bn_aggr(mv[:], st[:].rearrange("p a b -> p (a b)")).then_inc(st_done, 1)
                        eng.wait_ge(sd_done, T + 1)
                        nc.vector.reciprocal(rs[:], sd[:]).then_inc(st_done, 1)
                        eng.wait_ge(st_done, 3 * T + 3)
                        if not first:
                            eng.wait_ge(out_done[t], 32 * g)
                        nc.vector.tensor_scalar(xs[:, t, :], x_in_sb[t % 2][:], mv[:, 0:1], rs[:, 0:1], ALU.subtract,
                                                ALU.mult).then_inc(xs_done, 1)
                    lows(TG - 1, TG * g + TG - 1)

                def route(g, first=False):
                    n = [0]

                    def link(ins):
                        n[0] += 1
                        ins.then_inc(rt, 1)
                        eng.wait_ge(rt, RTS * g + n[0])

                    def row(c):
                        return c[:].rearrange("p (t o) -> p t o", o=1).to_broadcast([P, TG, E])

                    V = nc.vector
                    lg = lr[:, :, ER:ER + E]
                    eng.wait_ge(lr_done, TG * g + TG)
                    link(V.tensor_reduce(col[:], lg, AX.X, ALU.max))
                    link(V.tensor_tensor(sc[:], lg, row(col), ALU.subtract))
                    eng.wait_ge(ex_done, g + 1)
                    link(V.tensor_reduce(col[:], sc[:], AX.X, ALU.add))
                    link(V.reciprocal(col[:], col[:]))
                    link(V.tensor_tensor(sc[:], sc[:], row(col), ALU.mult))
                    for c, left in enumerate((sc, ta)):
                        link(V.tensor_reduce(top[c][:], left[:], AX.X, ALU.max))
                        link(V.tensor_tensor(tb[:], left[:], row(top[c]), ALU.is_equal))
                        link(V.tensor_tensor(tb[:], tb[:], order[:], ALU.mult))
                        link(V.tensor_reduce(col[:], tb[:], AX.X, ALU.max))
                        link(V.tensor_tensor(oh[c][:], tb[:], row(col), ALU.is_equal))
                        if c == 0:
                            link(V.scalar_tensor_tensor(out=ta[:], in0=oh[0][:], scalar=-2.0, in1=sc[:],
                                                        op0=ALU.mult, op1=ALU.add))
                    link(V.tensor_tensor(ta[:], oh[0][:], oh[1][:], ALU.add))
                    link(V.scalar_tensor_tensor(out=tb[:], in0=ta[:], scalar=gt[:, 0:1], in1=sc[:],
                                                op0=ALU.mult, op1=ALU.mult))
                    link(V.tensor_tensor(lr[:, :, 0:ER].rearrange("p t (e r) -> p t e r", e=E),
                                         lr[:, :, 0:ER].rearrange("p t (e r) -> p t e r", e=E),
                                         tb[:].rearrange("p t (e o) -> p t e o", o=1).to_broadcast([P, TG, E, R]),
                                         ALU.mult))
                    for c in range(2):
                        ins = V.tensor_scalar(keep.w[:, c, bass.ds(TG * g, TG)], top[c][:], gt[:, 0:1], None, ALU.mult)
                    eng.wait_ge(pos_done, g + 1)
                    link(V.tensor_tensor(sc[:], LT[:, 0:TG * E].rearrange("p (t e) -> p t e", t=TG),
                                         base[:].rearrange("p (o e) -> p o e", o=1).to_broadcast([P, TG, E]), ALU.add))
                    link(V.tensor_tensor(base[:], base[:], LT[:, TG * E:TG * E + E], ALU.add))
                    for c in range(2):
                        link(V.tensor_tensor(tb[:], oh[c][:], sc[:], ALU.mult))
                        link(V.tensor_reduce(col[:], tb[:], AX.X, ALU.add))
                        link(V.tensor_copy(place[:, c, :], col[:]))
                    link(V.tensor_copy(keep.row[:, :, bass.ds(TG * g, TG)], place[:]))
                    assert n[0] == RTS, n[0]
                    eng.wait_ge(lthi_done, g + 1)
                    nc.vector.tensor_tensor(keep.lt_lo[:, bass.ds(TG * P * g, TG * P)], LT[:],
                                            keep.lt_hi[:, bass.ds(TG * P * g, TG * P)].bitcast(F32),
                                            ALU.subtract).then_inc(ltlo_done, 1)

                def tables():
                    n = [0]

                    def link(ins):
                        n[0] += 1
                        ins.then_inc(tab, 1)
                        eng.wait_ge(tab, n[0])

                    V = nc.vector
                    I32 = mybir.dt.int32

                    def slots(a):
                        return a.rearrange("p (o e) -> p o e", o=1).to_broadcast([P, SLOTS, E])

                    def experts(a):
                        return a.rearrange("p (s o) -> p s o", o=1).to_broadcast([P, SLOTS, E])

                    link(V.tensor_scalar(pad[:], base[:], iota[:, 0:1], None, ALU.add))
                    link(V.tensor_tensor(nt[:], base[:], base0[:], ALU.subtract))
                    link(V.tensor_scalar(nti[:], nt[:], float(P - 1), float(P), ALU.add, ALU.max))
                    link(V.tensor_scalar(nti[:], nti[:], 7, None, ALU.logical_shift_right))
                    link(V.tensor_copy(nt[:], nti[:]))
                    link(V.memset(cum[:], 0.0))
                    for e in range(E):
                        link(V.tensor_tensor(cum[:, e + 1:e + 2], cum[:, e:e + 1], nt[:, e:e + 1], ALU.add))
                    start, end = cum[:, 0:E], cum[:, 1:E + 1]
                    link(V.tensor_tensor(big[0][:], experts(grid[:]), slots(start), ALU.is_ge))
                    link(V.tensor_tensor(big[1][:], experts(grid[:]), slots(end), ALU.is_ge))
                    link(V.tensor_tensor(big[2][:], big[0][:], big[1][:], ALU.subtract))
                    link(V.tensor_reduce(flat[0][:], big[1][:], AX.X, ALU.add))
                    link(V.tensor_scalar(flat[0][:], flat[0][:], float(E - 1), None, ALU.min))
                    link(V.tensor_copy(keep.table[:, 1, :], flat[0][:]))
                    link(V.tensor_scalar(keep.table[:, 2, :], keep.table[:, 1, :], 1, None, ALU.bitwise_and))
                    link(V.scalar_tensor_tensor(out=low_[:], in0=start, scalar=-float(P), in1=base0[:],
                                                op0=ALU.mult, op1=ALU.add))
                    link(V.tensor_scalar(low_[:], low_[:], -float(SPARE), None, ALU.add))
                    link(V.tensor_scalar(flat[1][:], grid[:], float(P), None, ALU.mult))
                    link(V.tensor_tensor(big[0][:], experts(flat[1][:]), slots(low_[:]), ALU.add))
                    link(V.tensor_tensor(big[0][:], big[0][:], big[2][:], ALU.mult))
                    link(V.tensor_reduce(flat[1][:], big[0][:], AX.X, ALU.add))
                    link(V.tensor_scalar(keep.table[:, 0, :], flat[1][:], float(SPARE), None, ALU.add))
                    link(V.scalar_tensor_tensor(out=low_[:], in0=start, scalar=float(P), in1=base0[:],
                                                op0=ALU.mult, op1=ALU.subtract))
                    link(V.tensor_copy(nt[:], low_[:]))
                    link(V.tensor_tensor(nt[:, 1:E], low_[:, 1:E], low_[:, 0:E - 1], ALU.subtract))
                    rows = flat[0][:, 0:2 * NT]
                    part = [b[:, 0:2 * NT, :] for b in big]
                    link(V.tensor_copy(rows, keep.row[:].rearrange("p c t -> p (c t)")))
                    link(V.tensor_tensor(part[0], rows.rearrange("p (s o) -> p s o", o=1).to_broadcast([P, 2 * NT, E]),
                                         base0[:].rearrange("p (o e) -> p o e", o=1).to_broadcast([P, 2 * NT, E]), ALU.is_ge))
                    link(V.tensor_tensor(part[0], part[0],
                                         nt[:].rearrange("p (o e) -> p o e", o=1).to_broadcast([P, 2 * NT, E]), ALU.mult))
                    link(V.tensor_reduce(flat[1][:, 0:2 * NT], part[0], AX.X, ALU.add))
                    link(V.tensor_tensor(rows, rows, flat[1][:, 0:2 * NT], ALU.add))
                    link(V.tensor_copy(keep.row[:].rearrange("p c t -> p (c t)"), rows))
                    link(V.tensor_copy(keep.ends[:], end))

                nc.vector.memset(epsc[:], EPS)
                nc.vector.memset(zero[:], 0.0).then_inc(misc, 1)
                eng.wait_ge(const_in, 144)
                eng.wait_ge(misc, 3)
                nc.vector.tensor_tensor(ag_lo[:], ag[:], ag_hi[:].bitcast(F32), ALU.subtract).then_inc(misc, 1)
                nc.vector.tensor_copy(base[:], base0[:]).then_inc(misc, 1)
                eng.wait_ge(misc, 5)
                sweep(0, first=True)
                route(0)
                with eng.Fori(1, NG) as g:
                    sweep(g)
                    route(g)
                tables()

            @block.tensor
            def _(eng):
                def transposes(t, T):
                    eng.wait_ge(xs_done, T + 1)
                    if not (isinstance(T, int) and T < 2):
                        eng.wait_ge(xlo_done, T - 1)
                    for c in range(NC):
                        mm = nc.tensor.transpose(XT[t % 2][:, c * P:(c + 1) * P], xs[:, t, c * P:(c + 1) * P], ident[:])
                    mm.then_inc(tr_done, 1)

                def project(t, T):
                    eng.wait_ge(xlo_done, T + 1)
                    if not (isinstance(T, int) and T < 2):
                        eng.wait_ge(lr_done, T - 1)
                    for c in range(NC):
                        out = LR[t % 2][:, 0:ER + E]
                        nc.tensor.matmul(out, xt_hi[t % 2][:, c, :], ag_hi[:, c, :], start=c == 0, stop=False)
                        nc.tensor.matmul(out, xt_hi[t % 2][:, c, :], ag_lo[:, c, :], start=False, stop=False)
                        mm = nc.tensor.matmul(out, xt_lo[t % 2][:, c, :], ag_hi[:, c, :], start=False, stop=c == NC - 1)
                    mm.then_inc(ag_done, 1)

                def count(g, first=False):
                    eng.wait_ge(rt, RTS * g + 17)
                    if not first:
                        eng.wait_ge(ltlo_done, g)
                    chosen = ta[:].rearrange("p t e -> p (t e)")
                    nc.tensor.matmul(LT[:, 0:TG * E], utri[:], chosen, start=True, stop=False)
                    for s in range(1, TG):
                        nc.tensor.matmul(LT[:, s * E:TG * E], ones[:], ta[:].rearrange("p t e -> p (t e)")[:, 0:(TG - s) * E],
                                         start=False, stop=s == TG - 1)
                    for t in range(TG):
                        mm = nc.tensor.matmul(LT[:, TG * E:TG * E + E], ones[:], ta[:, t, :], start=t == 0, stop=t == TG - 1)
                    mm.then_inc(pos_done, 1)

                def turn(g):
                    eng.wait_ge(rt, RTS * g + 21)
                    for t in range(TG):
                        mm = nc.tensor.transpose(LT[:, t * P:(t + 1) * P], lr[:, t, 0:ER], ident[:])
                    mm.then_inc(lt_done, 1)

                def group(g, first=False):
                    for t in range(TG):
                        transposes(t, TG * g + t)
                        if t:
                            project(t - 1, TG * g + t - 1)
                    project(TG - 1, TG * g + TG - 1)
                    count(g, first)
                    turn(g)

                eng.wait_ge(const_in, 144)
                eng.wait_ge(misc, 4)
                group(0, first=True)
                with eng.Fori(1, NG) as g:
                    group(g)


def experts_on_slots(nc, ctx0, keep, gu_d, dn_d, ident_d, sorted_d, made_d):
    ctx = ExitStack()
    with ctx:
        sb = lambda n, s, dt=F32: ctx.enter_context(nc.sbuf_tensor(n, s, dt))
        sem = lambda n: ctx.enter_context(nc.semaphore(n))
        ps = lambda n, s: ctx.enter_context(nc.psum_tensor(n, s, F32))
        ident = sb("ident3", [P, P])
        xr = [sb(f"xr{p}", [P, L]) for p in range(2)]
        xt_hi = [sb(f"xu_hi{p}", [P, NC, P], F32R) for p in range(2)]
        xt_lo = [sb(f"xu_lo{p}", [P, NC, P], F32R) for p in range(2)]
        gu_raw = sb("gu_raw", [P, NC, 2 * F])
        dn_raw = sb("dn_raw", [P, L])
        one = sb("one", [P, 1])
        gu_hi = sb("gu_hi", [P, 2, NC, 2 * F], F32R)
        gu_lo = sb("gu_lo", [P, 2, NC, 2 * F], F32R)
        dn_hi = sb("dn_hi", [P, 2, L], F32R)
        dn_lo = sb("dn_lo", [P, 2, L], F32R)
        h = [sb(f"h{p}", [P, F]) for p in range(2)]
        ht_hi = [sb(f"ht_hi{p}", [P, P], F32R) for p in range(2)]
        ht_lo = [sb(f"ht_lo{p}", [P, P], F32R) for p in range(2)]
        made = [sb(f"made{p}", [P, L]) for p in range(2)]
        XT = ps("XU", [P, L])
        GU = [ps(f"GU{p}", [P, HALF]) for p in range(2)]
        HT = ps("HT", [P, HALF])
        D = [ps(f"DD{c}", [P, HALF]) for c in range(2)]

        const_in = sem("const_in3")
        one_set = sem("one_set")
        xr_in = [sem(f"xr_in{p}") for p in range(2)]
        xt_ready, xhi_done, xlo_done = sem("xt_ready3"), sem("xhi_done3"), sem("xlo_done3")
        raw_in = sem("raw_in")
        whi_done = sem("whi_done")
        wlo_done = sem("wlo_done")
        gu_ready = sem("gu_ready")
        silu_done, h_done = sem("silu_done"), sem("h_done")
        ht_ready, hhi_done, hlo_done = sem("ht_ready"), sem("hhi_done"), sem("hlo_done")
        d_ready = sem("d_ready")
        d_out = [sem(f"d_out{c}") for c in range(2)]
        made_out = [sem(f"made_out{p}") for p in range(2)]

        def table(kind, k):
            return keep.table[0:1, kind, bass.ds(k, 1)]

        with nc.Block() as block:

            @block.sync
            def _(eng):
                def load(k, p):
                    if not (isinstance(k, int) and k < 2):
                        eng.wait_ge(xt_ready, k - 1)
                    r = eng.value_load(table(0, k), min_val=0, max_val=SPARE)
                    eng.dma_start(xr[p][:], sorted_d[bass.ds(r, P), :]).then_inc(xr_in[p], 16)

                def store(k, p):
                    eng.wait_ge(d_out[0], k + 1)
                    eng.wait_ge(d_out[1], k + 1)
                    eng.dma_start(made_d[k], made[p][:]).then_inc(made_out[p], 16)

                eng.dma_start(ident[:], ident_d).then_inc(const_in, 16)
                load(0, 0)
                load(1, 1)

                def slot(k, p, first=False, last=False):
                    if not last:
                        load(k + 2, p)
                    if not first:
                        store(k - 1, 1 - p)

                slot(0, 0, first=True)
                slot(1, 1)
                with eng.Fori(1, SLOTS // 2 - 1) as j:
                    for p in range(2):
                        slot(2 * j + p, p)
                slot(SLOTS - 2, 0, last=True)
                slot(SLOTS - 1, 1, last=True)
                store(SLOTS - 1, 1)
                for p in range(2):
                    eng.wait_ge(made_out[p], 16 * (SLOTS // 2))

            @block.gpsimd
            def _(eng):
                def fetch(e):
                    if e:
                        eng.wait_ge(wlo_done, 2 * e)
                    eng.dma_start(gu_raw[:], gu_d[e]).then_inc(raw_in, 16)
                    eng.dma_start(dn_raw[:], dn_d[e]).then_inc(raw_in, 16)

                def split(e):
                    eng.wait_ge(raw_in, 32 * e + 32)
                    if e >= 2:
                        eng.wait_ge(d_ready, eng.value_load(keep.ends[0:1, e - 2:e - 1], min_val=1, max_val=SLOTS))
                    nc.gpsimd.tensor_tensor(gu_hi[:, e % 2], gu_raw[:], view(one[:], [[0, NC], [0, 2 * F]]),
                                            ALU.mult).then_inc(whi_done, 1)
                    nc.gpsimd.tensor_tensor(dn_hi[:, e % 2], dn_raw[:], view(one[:], [[0, L]]),
                                            ALU.mult).then_inc(whi_done, 1)
                    for n, (hi, lo, raw) in enumerate(((gu_hi, gu_lo, gu_raw), (dn_hi, dn_lo, dn_raw))):
                        eng.wait_ge(whi_done, 2 * e + 1 + n)
                        nc.gpsimd.tensor_tensor(lo[:, e % 2], raw[:], hi[:, e % 2].bitcast(F32),
                                                ALU.subtract).then_inc(wlo_done, 1)

                nc.gpsimd.memset(one[:], 1.0).then_inc(one_set, 1)
                eng.wait_ge(one_set, 1)
                for e in range(E):
                    fetch(e)
                    split(e)

            @block.scalar
            def _(eng):
                def high(k, p):
                    eng.wait_ge(xt_ready, k + 1)
                    if not (isinstance(k, int) and k < 2):
                        eng.wait_ge(gu_ready, k - 1)
                    nc.scalar.copy(xt_hi[p][:], XT[:].rearrange("p (c n) -> p c n", c=NC)).then_inc(xhi_done, 1)

                def slot(k, p, first=False, last=False):
                    if not last:
                        high(k + 1, 1 - p)
                    eng.wait_ge(gu_ready, k + 1)
                    if not (isinstance(k, int) and k < 2):
                        eng.wait_ge(ht_ready, k - 1)
                    nc.scalar.activation(h[p][:], GU[p][:, 0:F], ACT.Silu).then_inc(silu_done, 1)
                    if not first:
                        copy_out(k - 1, 1 - p)
                    eng.wait_ge(ht_ready, k + 1)
                    nc.scalar.copy(ht_hi[p][:], HT[:, 0:P]).then_inc(hhi_done, 1)

                def copy_out(k, p):
                    eng.wait_ge(d_ready, k + 1)
                    if not (isinstance(k, int) and k < 2):
                        eng.wait_ge(made_out[p], 8 * (k - p))
                    nc.scalar.copy(made[p][:, 0:HALF], D[0][:]).then_inc(d_out[0], 1)

                high(0, 0)
                slot(0, 0, first=True)
                slot(1, 1)
                with eng.Fori(1, SLOTS // 2 - 1) as j:
                    for p in range(2):
                        slot(2 * j + p, p)
                slot(SLOTS - 2, 0)
                slot(SLOTS - 1, 1, last=True)
                copy_out(SLOTS - 1, 1)

            @block.vector
            def _(eng):
                def lows(k, p):
                    eng.wait_ge(xhi_done, k + 1)
                    nc.vector.tensor_tensor(xt_lo[p][:], XT[:].rearrange("p (c n) -> p c n", c=NC),
                                            xt_hi[p][:].bitcast(F32), ALU.subtract).then_inc(xlo_done, 1)

                def copy_out(k, p):
                    eng.wait_ge(d_ready, k + 1)
                    if not (isinstance(k, int) and k < 2):
                        eng.wait_ge(made_out[p], 8 * (k - p))
                    nc.vector.tensor_copy(made[p][:, HALF:L], D[1][:]).then_inc(d_out[1], 1)

                def slot(k, p, first=False, last=False):
                    if not last:
                        lows(k + 1, 1 - p)
                    eng.wait_ge(silu_done, k + 1)
                    nc.vector.tensor_tensor(h[p][:], GU[p][:, F:2 * F], h[p][:], ALU.mult).then_inc(h_done, 1)
                    if not first:
                        copy_out(k - 1, 1 - p)
                    eng.wait_ge(hhi_done, k + 1)
                    nc.vector.tensor_tensor(ht_lo[p][:], HT[:, 0:P], ht_hi[p][:].bitcast(F32),
                                            ALU.subtract).then_inc(hlo_done, 1)

                lows(0, 0)
                slot(0, 0, first=True)
                slot(1, 1)
                with eng.Fori(1, SLOTS // 2 - 1) as j:
                    for p in range(2):
                        slot(2 * j + p, p)
                slot(SLOTS - 2, 0)
                slot(SLOTS - 1, 1, last=True)
                copy_out(SLOTS - 1, 1)

            @block.tensor
            def _(eng):
                def transposes(k, p):
                    eng.wait_ge(xr_in[p], 8 * (k - p) + 16)
                    if not (isinstance(k, int) and k < 1):
                        eng.wait_ge(xlo_done, k)
                    for c in range(NC):
                        mm = nc.tensor.transpose(XT[:, c * P:(c + 1) * P], xr[p][:, c * P:(c + 1) * P], ident[:])
                    mm.then_inc(xt_ready, 1)

                def first_product(k, p, odd):
                    eng.wait_ge(xlo_done, k + 1)
                    if not (isinstance(k, int) and k < 2):
                        eng.wait_ge(h_done, k - 1)
                    out = GU[p][:, 0:2 * F]
                    for c in range(NC):
                        wh = gu_hi[:, bass.ds(odd, 1), c, :].rearrange("p o n -> p (o n)")
                        wl = gu_lo[:, bass.ds(odd, 1), c, :].rearrange("p o n -> p (o n)")
                        nc.tensor.matmul(out, xt_hi[p][:, c, :], wh, start=c == 0, stop=False)
                        nc.tensor.matmul(out, xt_lo[p][:, c, :], wh, start=False, stop=False)
                        mm = nc.tensor.matmul(out, xt_hi[p][:, c, :], wl, start=False, stop=c == NC - 1)
                    mm.then_inc(gu_ready, 1)

                def second_product(k, p, odd):
                    eng.wait_ge(hlo_done, k + 1)
                    if not (isinstance(k, int) and k < 1):
                        eng.wait_ge(d_out[0], k)
                        eng.wait_ge(d_out[1], k)
                    for c in range(2):
                        wh = dn_hi[:, bass.ds(odd, 1), c * HALF:(c + 1) * HALF].rearrange("p o n -> p (o n)")
                        wl = dn_lo[:, bass.ds(odd, 1), c * HALF:(c + 1) * HALF].rearrange("p o n -> p (o n)")
                        nc.tensor.matmul(D[c][:], ht_hi[p][:], wh, start=True, stop=False)
                        nc.tensor.matmul(D[c][:], ht_lo[p][:], wh, start=False, stop=False)
                        mm = nc.tensor.matmul(D[c][:], ht_hi[p][:], wl, start=False, stop=True)
                    mm.then_inc(d_ready, 1)

                def turn(k, p):
                    eng.wait_ge(h_done, k + 1)
                    if not (isinstance(k, int) and k < 1):
                        eng.wait_ge(hlo_done, k)
                    nc.tensor.transpose(HT[:, 0:P], h[p][:], ident[:]).then_inc(ht_ready, 1)

                def slot(k, p, first=False, last=False):
                    e = eng.value_load(table(1, k), min_val=0, max_val=E - 1)
                    odd = eng.value_load(table(2, k), min_val=0, max_val=1)
                    if not last:
                        transposes(k + 1, 1 - p)
                    eng.wait_ge(wlo_done, 2 * e + 2)
                    first_product(k, p, odd)
                    if not first:
                        second_product(k - 1, 1 - p, eng.value_load(table(2, k - 1), min_val=0, max_val=1))
                    turn(k, p)

                eng.wait_ge(const_in, 16)
                transposes(0, 0)
                slot(0, 0, first=True)
                slot(1, 1)
                with eng.Fori(1, SLOTS // 2 - 1) as j:
                    for p in range(2):
                        slot(2 * j + p, p)
                slot(SLOTS - 2, 0)
                slot(SLOTS - 1, 1, last=True)
                second_product(SLOTS - 1, 1, eng.value_load(table(2, SLOTS - 1), min_val=0, max_val=1))


def combine(nc, ctx0, keep, x1_d, lb_d, made_d, out_d):
    ctx = ExitStack()
    with ctx:
        sb = lambda n, s, dt=F32: ctx.enter_context(nc.sbuf_tensor(n, s, dt))
        sem = lambda n: ctx.enter_context(nc.semaphore(n))
        N = 3
        lb, lb_hi, lb_lo = sb("lb", [P, L]), sb("lb_hi", [P, L], F32R), sb("lb_lo", [P, L], F32R)
        acc = [sb(f"acc{p}", [P, L]) for p in range(2)]
        pick = [[sb(f"pick{c}{p}", [P, L]) for p in range(2)] for c in range(2)]
        D = [ctx.enter_context(nc.psum_tensor(f"DL{p}", [P, L], F32)) for p in range(2)]
        lb_in, lb_done = sem("lb_in"), sem("lb_done")
        acc_in = [sem(f"acc_in{p}") for p in range(2)]
        pick_in = [sem(f"pick_in{p}") for p in range(2)]
        d_ready = sem("d_ready4")
        added = sem("added")
        acc_out = [sem(f"acc_out{p}") for p in range(2)]

        with nc.Block() as block:

            @block.sync
            def _(eng):
                eng.dma_start(lb[:], lb_d).then_inc(lb_in, 16)
                for i in range(2):
                    eng.dma_start(acc[i][:], x1_d[i]).then_inc(acc_in[i], 16)

                def body(i, p, last=False):
                    eng.wait_ge(added, 3 * i + 3)
                    eng.dma_start(out_d[i], acc[p][:]).then_inc(acc_out[p], 16)
                    if not last:
                        eng.wait_ge(acc_out[p], 8 * (i - p) + 16)
                        eng.dma_start(acc[p][:], x1_d[i + 2]).then_inc(acc_in[p], 16)

                with eng.Fori(0, NT // 2 - 1) as j:
                    for p in range(2):
                        body(2 * j + p, p)
                body(NT - 2, 0, last=True)
                body(NT - 1, 1, last=True)
                for p in range(2):
                    eng.wait_ge(acc_out[p], 16 * (NT // 2))

            @block.gpsimd
            def _(eng):
                for i in range(NT):
                    p = i % 2
                    if i >= 2:
                        eng.wait_ge(added, 3 * (i - 2) + 3)
                    for c in range(2):
                        eng.indirect_dma_start(out=pick[c][p][:], out_offset=None, in_=made_d,
                                               in_offset=bass.IndirectOffsetOnAxis(ap=keep.row[:, c, i:i + 1], axis=0)) \
                            .then_inc(pick_in[p], 16)

            @block.scalar
            def _(eng):
                eng.wait_ge(lb_in, 16)
                nc.scalar.copy(lb_hi[:], lb[:]).then_inc(lb_done, 1)

            @block.vector
            def _(eng):
                eng.wait_ge(lb_done, 1)
                nc.vector.tensor_tensor(lb_lo[:], lb[:], lb_hi[:].bitcast(F32), ALU.subtract).then_inc(lb_done, 1)

                def body(i, p):
                    eng.wait_ge(acc_in[p], 8 * (i - p) + 16)
                    eng.wait_ge(d_ready, i + 1)
                    nc.vector.tensor_tensor(acc[p][:], D[p][:], acc[p][:], ALU.add).then_inc(added, 1)
                    for c in range(2):
                        eng.wait_ge(added, 3 * i + 1 + c)
                        if c == 0:
                            eng.wait_ge(pick_in[p], 16 * (i - p) + 32)
                        nc.vector.scalar_tensor_tensor(out=acc[p][:], in0=pick[c][p][:], scalar=keep.w[:, c, bass.ds(i, 1)],
                                                       in1=acc[p][:], op0=ALU.mult, op1=ALU.add).then_inc(added, 1)

                with eng.Fori(0, NT // 2) as j:
                    for p in range(2):
                        body(2 * j + p, p)

            @block.tensor
            def _(eng):
                eng.wait_ge(lb_done, 2)
                for i in range(NT):
                    p = i % 2
                    if i >= 2:
                        eng.wait_ge(added, 3 * (i - 2) + 1)
                    th, tl = keep.lt_hi[:, i * P:(i + 1) * P], keep.lt_lo[:, i * P:(i + 1) * P]
                    for c in range(2):
                        cols = slice(c * HALF, (c + 1) * HALF)
                        nc.tensor.matmul(D[p][:, cols], th, lb_hi[:, cols], start=True, stop=False)
                        nc.tensor.matmul(D[p][:, cols], tl, lb_hi[:, cols], start=False, stop=False)
                        mm = nc.tensor.matmul(D[p][:, cols], th, lb_lo[:, cols], start=False, stop=True)
                    mm.then_inc(d_ready, 1)


def build(nc, x, c, k, dskip, g1, g2, ident, gu, dn, lb, ag, order, utri, ones, base, iota, grid, out):
    kpad = nc.dram_tensor("kpad", [NH, KW], F32).ap()
    x1 = nc.dram_tensor("x1", [NT, P, L], F32).ap()
    sorted_rows = nc.dram_tensor("sorted_rows", [ROWS, L], F32).ap()
    made_rows = nc.dram_tensor("made_rows", [SLOTS, P, L], F32).ap()
    stage1(nc, x, c, k, dskip, g1, ident, kpad, x1)
    with ExitStack() as ctx:
        keep = Chosen(nc, ctx)
        route_tokens(nc, ctx, keep, x1, ag, g2, ident, order, utri, ones, base, iota, grid, sorted_rows)
        experts_on_slots(nc, ctx, keep, gu, dn, ident, sorted_rows, made_rows)
        combine(nc, ctx, keep, x1, lb, made_rows.rearrange("s p l -> (s p) l"), out)


def kernel(**inputs):
    import numpy as np
    import concourse.bacc as bacc
    from concourse.bass_utils import run_bass_kernel_spmd
    a = {n: np.asarray(v) for n, v in inputs.items()}

    def rows(t):
        return np.ascontiguousarray(t.reshape(B, NT, CT, L).transpose(1, 2, 0, 3)).reshape(NT, P, L)

    def model_major(t):
        return t.reshape(t.shape[0], t.shape[1], NC, P).transpose(0, 3, 2, 1)

    c = a["ctx_2048"].reshape(B, NT, HT, HD, NC, P).transpose(1, 5, 2, 4, 3, 0)[:, ::-1].reshape(NT, P, HT, NC, IB)
    k = a["L0_xattn_ssm_kernel"]
    arrays = {
        "x": rows(a["x"]),
        "c": np.ascontiguousarray(np.concatenate([c, c[..., :IB // 2]], axis=-1)),
        "k": np.ascontiguousarray(np.pad(k, ((0, 0), (P - 1, 1)))),
        "dskip": np.ascontiguousarray(a["L0_xattn_D"].reshape(NH, 1)),
        "g1": np.ascontiguousarray(np.broadcast_to(a["g_xattn"].reshape(1, 1), (P, 1))),
        "g2": np.ascontiguousarray(np.broadcast_to(a["g_ffn"].reshape(1, 1), (P, 1))),
        "ident": np.eye(P, dtype=np.float32),
        "gu": np.ascontiguousarray(np.concatenate([model_major(a["L0_ffn_gate_w"]), model_major(a["L0_ffn_up_w"])], axis=3)),
        "dn": np.ascontiguousarray(a["L0_ffn_down_w"].transpose(0, 2, 1)),
        "lb": np.ascontiguousarray(a["L0_ffn_lora_B"].transpose(0, 2, 1).reshape(ER, L)),
        "ag": np.ascontiguousarray(np.concatenate([model_major(a["L0_ffn_lora_A"].reshape(1, ER, L))[0],
                                                   a["L0_ffn_G"].reshape(NC, P, E).transpose(1, 0, 2)], axis=2)),
        "order": np.ascontiguousarray(np.broadcast_to(np.arange(E, 0, -1, dtype=np.float32), (P, TG, E))),
        "utri": np.triu(np.ones((P, P), np.float32), 1),
        "ones": np.ones((P, P), np.float32),
        "base": np.ascontiguousarray(np.broadcast_to(np.arange(E, dtype=np.float32) * RC, (P, E))),
        "iota": np.arange(P, dtype=np.float32).reshape(P, 1),
        "grid": np.ascontiguousarray(np.broadcast_to(np.arange(SLOTS, dtype=np.float32), (P, SLOTS))),
    }
    nc = bacc.Bacc("TRN2", target_bir_lowering=False, num_devices=1)
    ins = [nc.dram_tensor("in_" + n, v.shape, mybir.dt.from_np(v.dtype), kind="ExternalInput").ap() for n, v in arrays.items()]
    out = nc.dram_tensor("out", (NT, P, L), F32, kind="ExternalOutput").ap()
    build(nc, *ins, out)
    r = run_bass_kernel_spmd(nc, [{"in_" + n: v for n, v in arrays.items()}], core_ids=[0])
    y = r.results[0]["out"]
    return np.ascontiguousarray(y.reshape(NT, CT, B, L).transpose(2, 0, 1, 3)).reshape(B, CH, L)
```

```python
from contextlib import ExitStack

import concourse.bass as bass
from concourse import mybir

F32 = mybir.dt.float32
F32R = mybir.dt.float32r
ALU = mybir.AluOpType
ACT = mybir.ActivationFunctionType
AX = mybir.AxisListType

P = 128
B, CH, L = 8, 512, 1024
HD = 8
NH = CH // HD
HT = 2
CT = HT * HD
NT = CH // CT
NC = L // P
IB = HD * B
WR = IB + IB // 2
ND = 4
YC = ND * IB + IB // 2
FULL = ND * IB
SK = IB + B
ZS = 9
ZC = ZS * IB
ZB = 5 * IB
ZE = 8 * IB
KW = L + P
NP = NC // 2
ORDER = (1, 2, 0, 3)
EPS = 1e-5

HALF = 512
E, F, R = 8, 128, 16
ER = E * R
AC = ER + E
WC = NC * 2 * F + L
WQ = E * WC // NT
TOKENS = NT * P
GT = 4
NB = 24
LANDED = 32 * NT // E
SLOTS = 2 * TOKENS // P + E


def view(ap, dims, shift=0):
    return bass.AP(tensor=ap.tensor, offset=ap.offset + shift, ap=[list(ap.ap[0])] + [list(d) for d in dims])


class Constants:

    def __init__(self, nc, ctx, g_xattn, g_ffn, ident, order, utri, ones, iota, grid, number):
        sb = lambda n, s: ctx.enter_context(nc.sbuf_tensor("const_" + n, s, F32))
        self.g_xattn, self.g_ffn = sb("g_xattn", [P, 1]), sb("g_ffn", [P, 1])
        self.ident, self.utri, self.ones = sb("ident", [P, P]), sb("utri", [P, P]), sb("ones", [P, P])
        self.order = sb("order", [P, E])
        self.iota = sb("iota", [P, P])
        self.grid = sb("grid", [P, SLOTS])
        self.number = sb("number", [P, NT])
        self.first = [(self.ident, ident), (self.g_xattn, g_xattn)]
        self.later = [(self.g_ffn, g_ffn), (self.order, order), (self.utri, utri), (self.ones, ones), (self.iota, iota),
                      (self.grid, grid), (self.number, number)]


def attend(nc, lr, constants, x_d, c_d, k_d, dskip_d, ag_d, w_d, khi_d, klo_d, x1_d, normed_d, whi_d, wlo_d):
    ctx = ExitStack()
    with ctx:
        sb = lambda n, s, dt=F32: ctx.enter_context(nc.sbuf_tensor(n, s, dt))
        sem = lambda n: ctx.enter_context(nc.semaphore(n))
        x_nat = [sb(f"x_nat{p}", [P, L]) for p in range(2)]
        x_new = [sb(f"x_new{p}", [P, L]) for p in range(2)]
        xn = sb("xn", [P, L])
        cT = [sb(f"cT{p}", [P, HT, NC, WR]) for p in range(2)]
        qT = [sb(f"qT{p}", [P, HT, NC, WR]) for p in range(2)]
        kv = [sb(f"kv{h}", [P, NC, YC]) for h in range(HT)]
        kvhi = [sb(f"kvhi{h}", [P, NC, YC], F32R) for h in range(HT)]
        kvlo = [sb(f"kvlo{h}", [P, NC, YC], F32R) for h in range(HT)]
        t_hi = [sb(f"t_hi{h}", [P, L], F32R) for h in range(HT)]
        t_lo = [sb(f"t_lo{h}", [P, L], F32R) for h in range(HT)]
        oT = [sb(f"oT{p}", [P, NC, P]) for p in range(2)]
        z = [sb(f"z{p}", [P, 2, ZC]) for p in range(2)]
        ident, gate = constants.ident, constants.g_xattn
        krow = sb("krow", [NH, KW])
        krow_hi, krow_lo = sb("krow_hi", [NH, KW], F32R), sb("krow_lo", [NH, KW], F32R)
        n2 = [sb(f"n2{p}", [P, L]) for p in range(2)]
        n2_hi, n2_lo = sb("n2_hi", [P, NC, P], F32R), sb("n2_lo", [P, NC, P], F32R)
        ag = sb("ag", [P, NC, AC])
        p_small = sb("p_small", [P, AC])
        ag_parts = sb("ag_parts", [P, NC, 2, AC], F32R)
        w_raw, w_hi, w_lo = sb("w_raw", [P, WQ]), sb("w_hi", [P, WQ], F32R), sb("w_lo", [P, WQ], F32R)
        dcol = sb("dcol", [NH, 1])
        gt = sb("gt", [P, 1])
        epsc = sb("epsc", [P, 1])
        st = sb("st", [P, 2, 6])
        mv = sb("mv", [P, 2])
        sd = sb("sd", [P, 1])
        rs = sb("rs", [P, 1])
        st2 = sb("st2", [P, 2, 6])
        mv2 = sb("mv2", [P, 2])
        sd2 = sb("sd2", [P, 1])
        rs2 = sb("rs2", [P, 1])
        Y = [ctx.enter_context(nc.psum_tensor(f"Y{s}", [P, 2, HALF], F32)) for s in range(2)]
        OP = ctx.enter_context(nc.psum_tensor("OP", [P, L], F32))
        XP = ctx.enter_context(nc.psum_tensor("XP", [P, L], F32))

        later_in = sem("later_in")
        const_in = sem("const_in")
        k_in = sem("k_in")
        k_sum = sem("k_sum")
        khi_done, klo_done = sem("khi_done"), sem("klo_done")
        k_out = sem("k_out")
        ag_split = sem("ag_split")
        gate_ready = sem("gate_ready")
        x_in = [sem(f"x_in{p}") for p in range(2)]
        c_in = [sem(f"c_in{p}") for p in range(2)]
        t_in = [sem(f"t_in{h}") for h in range(HT)]
        kv_done = sem("kv_done")
        kvhi_done = sem("kvhi_done")
        kvlo_done = [sem(f"kvlo_done{h}") for h in range(HT)]
        y_ready = sem("y_ready")
        z_done = sem("z_done")
        z_zero = sem("z_zero")
        n2st_done = sem("n2st_done")
        n2sd_done = sem("n2sd_done")
        n2_done = sem("n2_done")
        n2_out = [sem(f"n2_out{p}") for p in range(2)]
        n2t_ready = sem("n2t_ready")
        n2hi_done, n2lo_done = sem("n2hi_done"), sem("n2lo_done")
        ag_ready = sem("ag_ready")
        small_done = sem("small_done")
        lr_done = sem("lr_done")
        w_in, whi_done, wlo_done, w_out = sem("w_in"), sem("whi_done"), sem("wlo_done"), sem("w_out")
        sum_done = sem("sum_done")
        o_ready = sem("o_ready")
        res_done = sem("res_done")
        x_out = [sem(f"x_out{p}") for p in range(2)]
        st_done = sem("st_done")
        sd_done = sem("sd_done")
        xn_done = sem("xn_done")
        xt_ready = sem("xt_ready")
        q_done = sem("q_done")

        def kernel_window(d, n):
            return bass.AP(tensor=d.tensor, offset=n * KW, ap=[[1, P], [1, L]])

        with nc.Block() as block:

            @block.sync
            def _(eng):
                eng.dma_start(krow[:], k_d).then_inc(k_in, 16)
                eng.dma_start(dcol[:], dskip_d).then_inc(k_in, 16)
                eng.dma_start(x_nat[0][:], x_d[0]).then_inc(x_in[0], 16)
                eng.dma_start(cT[0][:], c_d[0]).then_inc(c_in[0], 16)
                for s, d in constants.first:
                    eng.dma_start(s[:], d).then_inc(const_in, 16)
                eng.dma_start(ag[:], ag_d).then_inc(const_in, 16)
                eng.dma_start(w_raw[:], w_d[0]).then_inc(w_in, 16)
                eng.wait_ge(khi_done, 1)
                eng.dma_start(khi_d, krow_hi[:].bitcast(F32)).then_inc(k_out, 16)
                eng.wait_ge(klo_done, 1)
                eng.dma_start(klo_d, krow_lo[:].bitcast(F32)).then_inc(k_out, 16)
                eng.wait_ge(k_out, 32)

                def windows(n, h):
                    eng.dma_start(t_hi[h][:].bitcast(F32), kernel_window(khi_d, n)).then_inc(t_in[h], 16)
                    eng.dma_start(t_lo[h][:].bitcast(F32), kernel_window(klo_d, n)).then_inc(t_in[h], 16)

                for h in range(HT):
                    windows(h, h)
                eng.dma_start(cT[1][:], c_d[1]).then_inc(c_in[1], 16)
                for s, d in constants.later:
                    eng.dma_start(s[:], d).then_inc(later_in, 16)

                def body(i, p, first=False, last=False):
                    if not first and not last:
                        eng.wait_ge(kv_done, 4 * i)
                        eng.dma_start(cT[1 - p][:], c_d[i + 1]).then_inc(c_in[1 - p], 16)
                    if not first:
                        eng.wait_ge(res_done, i)
                    if not last:
                        eng.dma_start(x_nat[1 - p][:], x_d[i + 1]).then_inc(x_in[1 - p], 16)
                    if not first:
                        eng.dma_start(x1_d[i - 1], x_new[1 - p][:]).then_inc(x_out[1 - p], 16)
                    if not last:
                        eng.wait_ge(y_ready, 8 * i + 4)
                        windows(2 * i + 2, 0)
                    if not first:
                        eng.wait_ge(n2_done, i)
                        eng.dma_start(normed_d[i - 1], n2[1 - p][:]).then_inc(n2_out[1 - p], 16)
                    eng.wait_ge(wlo_done, i + 1)
                    if not last:
                        eng.dma_start(w_raw[:], w_d[i + 1]).then_inc(w_in, 16)
                    eng.dma_start(whi_d[i], w_hi[:].bitcast(F32)).then_inc(w_out, 16)
                    eng.dma_start(wlo_d[i], w_lo[:].bitcast(F32)).then_inc(w_out, 16)
                    if not last:
                        eng.wait_ge(y_ready, 8 * i + 8)
                        windows(2 * i + 3, 1)

                body(0, 0, first=True)
                body(1, 1)
                with eng.Fori(1, NT // 2 - 1) as k:
                    for p in range(2):
                        body(2 * k + p, p)
                body(NT - 2, 0)
                body(NT - 1, 1, last=True)
                eng.wait_ge(res_done, NT)
                eng.dma_start(x1_d[NT - 1], x_new[1][:]).then_inc(x_out[1], 16)
                eng.wait_ge(n2_done, NT)
                eng.dma_start(normed_d[NT - 1], n2[1][:]).then_inc(n2_out[1], 16)
                for p in range(2):
                    eng.wait_ge(x_out[p], 16 * (NT // 2))
                    eng.wait_ge(n2_out[p], 16 * (NT // 2))
                eng.wait_ge(w_out, 32 * NT)
                eng.wait_ge(later_in, 16 * len(constants.later))

            @block.gpsimd
            def _(eng):
                def products(n, h, half, p, have):
                    eng.wait_ge(c_in[p], have)
                    if not (isinstance(n, int) and n < HT):
                        eng.wait_ge(kvhi_done, 2 * (n - HT) + half + 1)
                        eng.wait_ge(kvlo_done[h], (n - HT - h) + half + 1)
                    c0 = half * (NC // 2)
                    cc = cT[p][:, h, c0:c0 + NC // 2, 0:IB]
                    o = kv[h][:, c0:c0 + NC // 2, 0:IB]
                    nc.gpsimd.tensor_tensor(view(o, [[YC, NC // 2], [IB, ND], [1, IB]]),
                                            view(cc, [[WR, NC // 2], [0, ND], [1, IB]]),
                                            view(cc, [[WR, NC // 2], [B, ND], [1, IB]]), ALU.mult)
                    nc.gpsimd.tensor_tensor(kv[h][:, c0:c0 + NC // 2, FULL:YC],
                                            cT[p][:, h, c0:c0 + NC // 2, 0:IB // 2],
                                            cT[p][:, h, c0:c0 + NC // 2, IB // 2:IB], ALU.mult).then_inc(kv_done, 1)

                def low_kv(n, h):
                    for half in range(2):
                        eng.wait_ge(kvhi_done, 2 * n + half + 1)
                        c0 = half * (NC // 2)
                        nc.gpsimd.tensor_tensor(kvlo[h][:, c0:c0 + NC // 2, :], kv[h][:, c0:c0 + NC // 2, :],
                                                kvhi[h][:, c0:c0 + NC // 2, :].bitcast(F32),
                                                ALU.subtract).then_inc(kvlo_done[h], 1)

                def low_w(i):
                    eng.wait_ge(whi_done, i + 1)
                    nc.gpsimd.tensor_tensor(w_lo[:], w_raw[:], w_hi[:].bitcast(F32), ALU.subtract).then_inc(wlo_done, 1)

                def head(i, p, h, have):
                    products(2 * i + h, h, 0, p, have)
                    products(2 * i + h, h, 1, p, have)
                    low_kv(2 * i + h, h)

                head(0, 0, 0, 16)

                def body(i, p, k, last=False):
                    low_w(i)
                    head(i, p, 1, 16 * (k + 1))
                    if not last:
                        head(i + 1, 1 - p, 0, 16 * (k + 1 + p))

                body(0, 0, 0)
                body(1, 1, 0)
                with eng.Fori(1, NT // 2 - 1) as k:
                    for p in range(2):
                        body(2 * k + p, p, k)
                body(NT - 2, 0, NT // 2 - 1)
                body(NT - 1, 1, NT // 2 - 1, last=True)

            @block.scalar
            def _(eng):
                def high_kv(n, h):
                    for half in range(2):
                        eng.wait_ge(kv_done, 2 * n + half + 1)
                        if half == 0 and not (isinstance(n, int) and n < HT):
                            eng.wait_ge(y_ready, NP * (n - 1))
                        c0 = half * (NC // 2)
                        nc.scalar.copy(kvhi[h][:, c0:c0 + NC // 2, :],
                                       kv[h][:, c0:c0 + NC // 2, :]).then_inc(kvhi_done, 1)

                def root(i):
                    eng.wait_ge(st_done, 3 * i + 2)
                    nc.scalar.activation(sd[:], mv[:, 1:2], ACT.Sqrt, bias=epsc[:, 0:1]).then_inc(sd_done, 1)

                def take_q(i, p):
                    eng.wait_ge(xt_ready, i + 1)
                    if not (isinstance(i, int) and i < 2):
                        eng.wait_ge(z_done, 8 * (i - 1))
                    src = XP[:]
                    nc.scalar.copy(qT[p][:, :, :, 0:IB], view(src, [[IB, HT], [P, NC], [1, IB]]))
                    nc.scalar.copy(qT[p][:, :, :, IB:WR], view(src, [[IB, HT], [P, NC], [1, IB // 2]])) \
                        .then_inc(q_done, 1)

                def high_w(i):
                    eng.wait_ge(w_in, 16 * i + 16)
                    if not (isinstance(i, int) and i < 1):
                        eng.wait_ge(w_out, 32 * i)
                    nc.scalar.copy(w_hi[:], w_raw[:]).then_inc(whi_done, 1)

                def root2(i):
                    eng.wait_ge(n2st_done, 3 * i + 2)
                    nc.scalar.activation(sd2[:], mv2[:, 1:2], ACT.Sqrt, bias=epsc[:, 0:1]).then_inc(n2sd_done, 1)

                def high_n2(i):
                    eng.wait_ge(n2t_ready, i + 1)
                    if not (isinstance(i, int) and i < 1):
                        eng.wait_ge(ag_ready, i)
                    nc.scalar.copy(n2_hi[:], XP[:].rearrange("p (c n) -> p c n", c=NC)).then_inc(n2hi_done, 1)

                def take_small(i):
                    eng.wait_ge(ag_ready, i + 1)
                    if not (isinstance(i, int) and i < 1):
                        eng.wait_ge(lr_done, i)
                    nc.scalar.copy(p_small[:], XP[:, AC:2 * AC]).then_inc(small_done, 1)

                eng.wait_ge(k_sum, 1)
                nc.scalar.copy(krow_hi[:], krow[:]).then_inc(khi_done, 1)
                eng.wait_ge(const_in, 48)
                nc.scalar.activation(gt[:], gate[:], ACT.Tanh).then_inc(gate_ready, 1)
                nc.scalar.copy(ag_parts[:, :, 0, :], ag[:]).then_inc(ag_split, 1)
                root(0)
                high_kv(0, 0)
                take_q(0, 0)

                def body(i, p, k, first=False, last=False):
                    if not (isinstance(i, int) and i < 2):
                        high_n2(i - 2)
                    high_w(i)
                    high_kv(2 * i + 1, 1)
                    if not (isinstance(i, int) and i < 2):
                        take_small(i - 2)
                    if not first:
                        root2(i - 1)
                    if not last:
                        root(i + 1)
                        high_kv(2 * i + 2, 0)
                    if not last:
                        take_q(i + 1, 1 - p)

                body(0, 0, 0, first=True)
                body(1, 1, 0)
                with eng.Fori(1, NT // 2 - 1) as k:
                    for p in range(2):
                        body(2 * k + p, p, k)
                body(NT - 2, 0, NT // 2 - 1)
                body(NT - 1, 1, NT // 2 - 1, last=True)
                high_n2(NT - 2)
                take_small(NT - 2)
                root2(NT - 1)
                high_n2(NT - 1)
                take_small(NT - 1)

            @block.vector
            def _(eng):
                def multiply(i, p, h, n):
                    s, r = n % 2, ORDER[n]
                    idx = 8 * i + 4 * h + n
                    eng.wait_ge(y_ready, idx + 1)
                    if h == 0 and n == 0:
                        eng.wait_ge(q_done, i + 1)
                    if not (isinstance(i, int) and i == 0 and h == 0 and n < 2):
                        eng.wait_ge(sum_done, idx - 1)
                    y = Y[s][:, :, 0:YC]
                    q = qT[p][:, h, 2 * r:2 * r + 2, :]
                    zz = z[s][:]
                    nc.vector.tensor_tensor(view(zz, [[ZC, 2], [SK, ND], [1, IB]]),
                                            view(y, [[HALF, 2], [IB, ND], [1, IB]]),
                                            view(q, [[WR, 2], [0, ND], [1, IB]]), ALU.mult)
                    nc.vector.tensor_tensor(view(zz, [[ZC, 2], [IB, ND - 1], [1, IB]], ZB),
                                            view(y, [[HALF, 2], [IB, ND - 1], [1, IB]], IB),
                                            view(q, [[WR, 2], [B, ND - 1], [1, IB]], B), ALU.mult)
                    nc.vector.tensor_tensor(view(zz, [[ZC, 2], [IB // 2, 2], [1, IB // 2]], ZE),
                                            view(y, [[HALF, 2], [0, 2], [1, IB // 2]], FULL),
                                            view(q, [[WR, 2], [IB // 2, 2], [1, IB // 2]], IB // 2),
                                            ALU.mult).then_inc(z_done, 1)

                def total(i, p, h, n):
                    s, r = n % 2, ORDER[n]
                    eng.wait_ge(z_done, 8 * i + 4 * h + n + 1)
                    if h == 0 and n == 0 and not (isinstance(i, int) and i < 2):
                        eng.wait_ge(o_ready, i - 1)
                    nc.vector.tensor_reduce(oT[p][:, 2 * r:2 * r + 2, h * IB:(h + 1) * IB],
                                            view(z[s][:], [[ZC, 2], [1, IB], [IB, ZS]]), AX.X,
                                            ALU.add).then_inc(sum_done, 1)

                def stats(i, p, have):
                    eng.wait_ge(x_in[p], have)
                    if not (isinstance(i, int) and i < 1):
                        eng.wait_ge(xn_done, i)
                    nc.vector.bn_stats(st[:, 0, :], x_nat[p][:, 0:HALF])
                    nc.vector.bn_stats(st[:, 1, :], x_nat[p][:, HALF:L]).then_inc(st_done, 1)

                def aggregate(i):
                    nc.vector.bn_aggr(mv[:], st[:].rearrange("p a b -> p (a b)")).then_inc(st_done, 1)

                def invert(i):
                    eng.wait_ge(sd_done, i + 1)
                    nc.vector.reciprocal(rs[:], sd[:]).then_inc(st_done, 1)

                def normalize(i, p):
                    eng.wait_ge(st_done, 3 * i + 3)
                    if not (isinstance(i, int) and i < 1):
                        eng.wait_ge(xt_ready, i)
                    nc.vector.tensor_scalar(xn[:], x_nat[p][:], mv[:, 0:1], rs[:, 0:1], ALU.subtract,
                                            ALU.mult).then_inc(xn_done, 1)

                def residual(i, p):
                    eng.wait_ge(o_ready, i + 1)
                    if not (isinstance(i, int) and i < 2):
                        eng.wait_ge(x_out[p], stored[p](i))
                    nc.vector.scalar_tensor_tensor(out=x_new[p][:], in0=OP[:], scalar=gt[:, 0:1],
                                                   in1=x_nat[p][:], op0=ALU.mult,
                                                   op1=ALU.add).then_inc(res_done, 1)

                def stats2(i, p):
                    eng.wait_ge(res_done, i + 1)
                    if not (isinstance(i, int) and i < 1):
                        eng.wait_ge(n2_done, i)
                    nc.vector.bn_stats(st2[:, 0, :], x_new[p][:, 0:HALF])
                    nc.vector.bn_stats(st2[:, 1, :], x_new[p][:, HALF:L]).then_inc(n2st_done, 1)

                def aggregate2():
                    nc.vector.bn_aggr(mv2[:], st2[:].rearrange("p a b -> p (a b)")).then_inc(n2st_done, 1)

                def invert2(i):
                    eng.wait_ge(n2sd_done, i + 1)
                    nc.vector.reciprocal(rs2[:], sd2[:]).then_inc(n2st_done, 1)

                def normalize2(i, p):
                    eng.wait_ge(n2st_done, 3 * i + 3)
                    if not (isinstance(i, int) and i < 2):
                        eng.wait_ge(n2_out[p], stored[p](i))
                        eng.wait_ge(n2t_ready, i - 1)
                    nc.vector.tensor_scalar(n2[p][:], x_new[p][:], mv2[:, 0:1], rs2[:, 0:1], ALU.subtract,
                                            ALU.mult).then_inc(n2_done, 1)

                def low_n2(i):
                    eng.wait_ge(n2hi_done, i + 1)
                    nc.vector.tensor_tensor(n2_lo[:], XP[:].rearrange("p (c n) -> p c n", c=NC), n2_hi[:].bitcast(F32),
                                            ALU.subtract).then_inc(n2lo_done, 1)

                def take_lr(i):
                    eng.wait_ge(ag_ready, i + 1)
                    at = slice(i, i + 1) if isinstance(i, int) else bass.ds(i, 1)
                    to = lr[:, at, :].rearrange("p o n -> p (o n)")
                    eng.wait_ge(small_done, i + 1)
                    nc.vector.tensor_tensor(to, XP[:, 0:AC], p_small[:], ALU.add).then_inc(lr_done, 1)

                stored = [lambda i: 8 * i, lambda i: 8 * i - 8]

                nc.vector.memset(epsc[:], EPS)
                nc.vector.memset(z[0][:], 0.0)
                nc.vector.memset(z[1][:], 0.0).then_inc(z_zero, 1)
                eng.wait_ge(k_in, 32)
                nc.vector.tensor_tensor(krow[:, P - 1:P], krow[:, P - 1:P], dcol[:], ALU.add).then_inc(k_sum, 1)
                eng.wait_ge(khi_done, 1)
                nc.vector.tensor_tensor(krow_lo[:], krow[:], krow_hi[:].bitcast(F32), ALU.subtract).then_inc(klo_done, 1)
                eng.wait_ge(z_zero, 1)
                stats(0, 0, 16)
                eng.wait_ge(st_done, 1)
                aggregate(0)
                invert(0)
                normalize(0, 0)
                eng.wait_ge(gate_ready, 1)
                eng.wait_ge(ag_split, 1)
                nc.vector.tensor_tensor(ag_parts[:, :, 1, :], ag[:], ag_parts[:, :, 0, :].bitcast(F32), ALU.subtract).then_inc(ag_split, 1)

                def body(i, p, k, first=False, last=False):
                    early = isinstance(i, int) and i < 2
                    if not first:
                        total(i - 1, 1 - p, 1, 3)
                    multiply(i, p, 0, 0)
                    if not early:
                        low_n2(i - 2)
                    total(i, p, 0, 0)
                    multiply(i, p, 0, 1)
                    if not first:
                        residual(i - 1, 1 - p)
                    total(i, p, 0, 1)
                    multiply(i, p, 0, 2)
                    if not first:
                        stats2(i - 1, 1 - p)
                    if not last:
                        stats(i + 1, 1 - p, 16 * (k + 1 + p))
                    if not first:
                        eng.wait_ge(n2st_done, 3 * i - 2)
                    if not last:
                        eng.wait_ge(st_done, 3 * i + 4)
                    total(i, p, 0, 2)
                    if not first:
                        aggregate2()
                    if not last:
                        aggregate(i + 1)
                    if not early:
                        take_lr(i - 2)
                    multiply(i, p, 0, 3)
                    total(i, p, 0, 3)
                    multiply(i, p, 1, 0)
                    if not first:
                        invert2(i - 1)
                        normalize2(i - 1, 1 - p)
                    if not last:
                        invert(i + 1)
                        normalize(i + 1, 1 - p)
                    total(i, p, 1, 0)
                    multiply(i, p, 1, 1)
                    total(i, p, 1, 1)
                    multiply(i, p, 1, 2)
                    total(i, p, 1, 2)
                    multiply(i, p, 1, 3)

                body(0, 0, 0, first=True)
                body(1, 1, 0)
                with eng.Fori(1, NT // 2 - 1) as k:
                    for p in range(2):
                        body(2 * k + p, p, k)
                body(NT - 2, 0, NT // 2 - 1)
                body(NT - 1, 1, NT // 2 - 1, last=True)
                total(NT - 1, 1, 1, 3)
                residual(NT - 1, 1)
                low_n2(NT - 2)
                stats2(NT - 1, 1)
                take_lr(NT - 2)
                eng.wait_ge(n2st_done, 3 * NT - 2)
                aggregate2()
                invert2(NT - 1)
                normalize2(NT - 1, 1)
                low_n2(NT - 1)
                take_lr(NT - 1)

            @block.tensor
            def _(eng):
                def conv(i, h, n):
                    idx = 8 * i + 4 * h + n
                    s2, r = n % 2, ORDER[n]
                    if n == 0:
                        eng.wait_ge(t_in[h], 32 * i + 32)
                        eng.wait_ge(kvlo_done[h], 2 * i + 1)
                    if n == 1:
                        eng.wait_ge(kvlo_done[h], 2 * i + 2)
                    if not (isinstance(i, int) and i == 0 and h == 0 and n < 2):
                        eng.wait_ge(z_done, idx - 1)
                    for a in range(2):
                        c = 2 * r + a
                        for s in range(c + 1):
                            w = slice((c - s) * P, (c - s + 1) * P)
                            for t, m in ((t_hi, kvhi), (t_hi, kvlo), (t_lo, kvhi)):
                                mm = nc.tensor.matmul(Y[s2][:, a, 0:YC], t[h][:, w], m[h][:, s, :],
                                                      start=(s == 0 and t is t_hi and m is kvhi),
                                                      stop=(s == c and t is t_lo))
                    mm.then_inc(y_ready, 1)

                def transpose_x(i):
                    eng.wait_ge(xn_done, i + 1)
                    if not (isinstance(i, int) and i < 1):
                        eng.wait_ge(q_done, i)
                    if not (isinstance(i, int) and i < 3):
                        eng.wait_ge(lr_done, i - 2)
                    for c in range(NC):
                        mm = nc.tensor.transpose(XP[:, c * P:(c + 1) * P], xn[:, c * P:(c + 1) * P], ident[:])
                    mm.then_inc(xt_ready, 1)

                def transpose_o(i, p):
                    eng.wait_ge(sum_done, 8 * i + 8)
                    if not (isinstance(i, int) and i < 1):
                        eng.wait_ge(res_done, i)
                    for c in range(NC):
                        mm = nc.tensor.transpose(OP[:, c * P:(c + 1) * P], oT[p][:, c, :], ident[:])
                    mm.then_inc(o_ready, 1)

                def transpose_n2(i, p):
                    eng.wait_ge(n2_done, i + 1)
                    eng.wait_ge(q_done, min(i + 3, NT) if isinstance(i, int) else i + 3)
                    for c in range(NC):
                        mm = nc.tensor.transpose(XP[:, c * P:(c + 1) * P], n2[p][:, c * P:(c + 1) * P], ident[:])
                    mm.then_inc(n2t_ready, 1)

                def project(i):
                    eng.wait_ge(n2lo_done, i + 1)
                    for c in range(NC):
                        nc.tensor.matmul(XP[:, 0:2 * AC], n2_hi[:, c, :], ag_parts[:, c].rearrange("p o n -> p (o n)"),
                                         start=c == 0, stop=False)
                        mm = nc.tensor.matmul(XP[:, 0:AC], n2_lo[:, c, :], ag_parts[:, c, 0, :], start=False, stop=c == NC - 1)
                    mm.then_inc(ag_ready, 1)

                eng.wait_ge(const_in, 48)
                transpose_x(0)

                def body(i, p, first=False, last=False):
                    for n in range(NP):
                        conv(i, 0, n)
                        if n == 1 and not first:
                            transpose_o(i - 1, 1 - p)
                        if n == 2 and not (isinstance(i, int) and i < 2):
                            project(i - 2)
                    for n in range(NP):
                        conv(i, 1, n)
                        if n == 2 and not last:
                            transpose_x(i + 1)
                    if not first:
                        transpose_n2(i - 1, 1 - p)

                body(0, 0, first=True)
                eng.wait_ge(ag_split, 2)
                body(1, 1)
                with eng.Fori(1, NT // 2 - 1) as k:
                    for p in range(2):
                        body(2 * k + p, p)
                body(NT - 2, 0)
                body(NT - 1, 1, last=True)
                transpose_o(NT - 1, 1)
                project(NT - 2)
                eng.wait_ge(lr_done, NT - 1)
                transpose_n2(NT - 1, 1)
                project(NT - 1)


class Chosen:

    def __init__(self, nc, ctx):
        sb = lambda n, s, dt=F32: ctx.enter_context(nc.sbuf_tensor(n, s, dt))
        self.lt_hi = sb("lt_hi", [P, TOKENS], F32R)
        self.lt_lo = sb("lt_lo", [P, TOKENS], F32R)
        self.row = sb("row", [P, 2, NT], mybir.dt.uint32)
        self.w = sb("wsel", [P, 2, NT])
        self.token = sb("token", [P, SLOTS], mybir.dt.uint32)
        self.table = sb("table", [P, 2, SLOTS], mybir.dt.int32)
        self.ends = sb("ends", [P, E], mybir.dt.int32)


class Weights:

    def __init__(self, nc, ctx):
        sb = lambda n, s, dt=F32: ctx.enter_context(nc.sbuf_tensor(n, s, dt))
        self.hi = sb("wt_hi", [P, 2, WC], F32R)
        self.lo = sb("wt_lo", [P, 2, WC], F32R)
        self.landed = ctx.enter_context(nc.semaphore("weights_landed"))

    def load(self, eng, whi_d, wlo_d, e, singly=False):
        for q in range(NT // E):
            cols = slice(q * WQ, (q + 1) * WQ)
            for part, d in ((self.hi, whi_d), (self.lo, wlo_d)):
                eng.dma_start(part[:, e % 2, cols].bitcast(F32), d[NT // E * e + q]).then_inc(self.landed, 16)
            if singly:
                eng.wait_ge(self.landed, LANDED * e + 32 * (q + 1))


class Base:

    def __init__(self, nc, ctx, lr, weights, rows):
        sb = lambda n, s, dt=F32: ctx.enter_context(nc.sbuf_tensor(n, s, dt))
        sem = lambda n: ctx.enter_context(nc.semaphore(n))
        own = NB - NT * AC // L - 2 * (WC // L)
        self.tiles = sb("base", [P, own, L])
        self.at = [self.tiles[:, t, :] for t in range(own)]
        self.at += [view(lr[:], [[1, L]], t * L) for t in range(NT * AC // L)]
        self.at += [part[:, (E - 2) % 2, t * L:(t + 1) * L].bitcast(F32) for part in (weights.hi, weights.lo) for t in range(WC // L)]
        self.at += [part[:, (E - 1) % 2, t * L:(t + 1) * L].bitcast(F32) for part in (weights.hi, weights.lo) for t in range(WC // L)]
        self.at += [b[:] for b in rows.buffer]
        self.late = [sem(f"late_in{i}") for i in range(NT - NB)]
        self.lb, self.lb_hi, self.lb_lo = sb("lb", [P, L]), sb("lb_hi", [P, L], F32R), sb("lb_lo", [P, L], F32R)
        self.landed, self.lb_in, self.lb_high = sem("base_landed"), sem("lb_in"), sem("lb_high")

    def load(self, eng, x1_d, tiles):
        for t in tiles:
            eng.dma_start(self.at[t], x1_d[t]).then_inc(self.landed, 16)
            eng.wait_ge(self.landed, 16 * t + 16)


class Rows:

    def __init__(self, nc, ctx):
        self.buffer = [ctx.enter_context(nc.sbuf_tensor(f"slot_rows{p}", [P, L], F32)) for p in range(2)]
        self.landed = [ctx.enter_context(nc.semaphore(f"rows_landed{p}")) for p in range(2)]

    def gather(self, eng, keep, normed_d, k):
        eng.indirect_dma_start(out=self.buffer[k % 2][:], out_offset=None, in_=normed_d,
                               in_offset=bass.IndirectOffsetOnAxis(ap=keep.token[:, k:k + 1], axis=0)) \
            .then_inc(self.landed[k % 2], 16)


def route_tokens(nc, keep, weights, rows, lr, constants, normed_d, whi_d, wlo_d):
    ctx = ExitStack()
    with ctx:
        sb = lambda n, s, dt=F32: ctx.enter_context(nc.sbuf_tensor(n, s, dt))
        sem = lambda n: ctx.enter_context(nc.semaphore(n))
        ps = lambda n, s: ctx.enter_context(nc.psum_tensor(n, s, F32))
        I32 = mybir.dt.int32
        ident, utri, ones = constants.ident, constants.utri, constants.ones
        utri_r, ones_r = sb("utri_r", [P, P], F32R), sb("ones_r", [P, P], F32R)
        order, iota, grid, number = constants.order, constants.iota, constants.grid, constants.number
        gate, gt = constants.g_ffn, sb("gt2", [P, 1])
        sc, ta, tb = sb("sc", [P, NT, E]), sb("ta", [P, NT, E]), sb("tb", [P, NT, E])
        wt = sb("wt", [P, NT, E])
        oh = [sb(f"oh{c}", [P, NT, E]) for c in range(2)]
        chosen = sb("chosen", [P, NT, E], F32R)
        sums = sb("sums", [P, E], F32R)
        col, top = sb("col", [P, NT]), [sb(f"top{c}", [P, NT]) for c in range(2)]
        nt, cum = sb("nt", [P, E]), sb("cum", [P, E + 1])
        nti = sb("nti", [P, E], I32)
        place, slot_i, row_i = sb("place", [P, 2, NT]), sb("slot_i", [P, 2, NT], I32), sb("row_i", [P, 2, NT], I32)
        slot_f, row_f = sb("slot_f", [P, 2, NT]), sb("row_f", [P, 2, NT])
        is_row = sb("is_row", [P, 2, NT, P], F32R)
        is_slot = sb("is_slot", [P, 2, NT, SLOTS])
        groups = sb("groups", [P, NT // GT, E], F32R)
        slot_number = sb("slot_number", [P, 2, NT, SLOTS], F32R)
        ended = sb("ended", [P, SLOTS, E])
        expert = sb("expert", [P, SLOTS])
        CNT, IDX = ps("CNT", [P, HALF]), ps("IDX", [P, HALF])
        TOT = CNT[:, NT * E:(NT + 1) * E]
        LT = [ps(f"LT{p}", [P, L]) for p in range(3)]
        LG = NT * P // L

        misc = sem("misc")
        rt = sem("rt")
        ex_done = sem("ex_done")
        cnt_done = sem("cnt_done")
        num_done = sem("num_done")
        token_done = sem("token_done")
        idx_done = sem("idx_done")
        lw_done = sem("lw_done")
        lt_done = sem("lt_done")
        lthi_done, ltlo_done = sem("lthi_done"), sem("ltlo_done")
        at = {}

        with nc.Block() as block:

            @block.sync
            def _(eng):
                for e in range(2):
                    weights.load(eng, whi_d, wlo_d, e)
                eng.wait_ge(weights.landed, 2 * LANDED)

            @block.vector
            def _(eng):
                n = [0]
                V = nc.vector

                def link(ins, name=None):
                    n[0] += 1
                    at[name] = n[0]
                    ins.then_inc(rt, 1)
                    eng.wait_ge(rt, n[0])

                def step(ins, name):
                    n[0] += 1
                    at[name] = n[0]
                    ins.then_inc(rt, 1)

                def low(g):
                    eng.wait_ge(lthi_done, g + 1)
                    V.tensor_tensor(keep.lt_lo[:, L * g:L * (g + 1)], LT[g % 3][:], keep.lt_hi[:, L * g:L * (g + 1)].bitcast(F32),
                                    ALU.subtract).then_inc(ltlo_done, 1)

                def tokens(c):
                    return c.rearrange("p (t o) -> p t o", o=1).to_broadcast([P, NT, E])

                def experts(c):
                    return c.rearrange("p (o e) -> p o e", o=1).to_broadcast([P, NT, E])

                lg = lr[:, :, ER:AC]
                link(V.tensor_reduce(col[:], lg, AX.X, ALU.max))
                link(V.tensor_tensor(sc[:], lg, tokens(col[:]), ALU.subtract), "logits")
                eng.wait_ge(ex_done, 1)
                link(V.tensor_reduce(col[:], sc[:], AX.X, ALU.add))
                link(V.reciprocal(col[:], col[:]))
                link(V.tensor_tensor(sc[:], sc[:], tokens(col[:]), ALU.mult))
                for c, left in enumerate((sc, ta)):
                    link(V.tensor_reduce(top[c][:], left[:], AX.X, ALU.max))
                    link(V.tensor_tensor(tb[:], left[:], tokens(top[c][:]), ALU.is_equal))
                    link(V.tensor_tensor(tb[:], tb[:], experts(order[:]), ALU.mult))
                    link(V.tensor_reduce(col[:], tb[:], AX.X, ALU.max))
                    link(V.tensor_tensor(oh[c][:], tb[:], tokens(col[:]), ALU.is_equal))
                    if c == 0:
                        link(V.scalar_tensor_tensor(out=ta[:], in0=oh[0][:], scalar=-2.0, in1=sc[:],
                                                    op0=ALU.mult, op1=ALU.add))
                link(V.tensor_tensor(chosen[:], oh[0][:], oh[1][:], ALU.add))
                with nc.allow_low_precision("counts up to 32 are exact"):
                    link(V.tensor_reduce(groups[:], chosen[:].bitcast(F32).rearrange("p (g t) e -> p g e t", t=GT), AX.X, ALU.add))
                    link(V.tensor_reduce(sums[:], groups[:].bitcast(F32).rearrange("p g e -> p e g"), AX.X, ALU.add), "chosen")
                eng.wait_ge(misc, 3)
                link(V.scalar_tensor_tensor(out=wt[:], in0=chosen[:].bitcast(F32), scalar=gt[:, 0:1], in1=sc[:],
                                            op0=ALU.mult, op1=ALU.mult), "weights")
                for c in range(2):
                    V.tensor_scalar(keep.w[:, c, :], top[c][:], gt[:, 0:1], None, ALU.mult)
                link(V.memset(cum[:], 0.0))
                eng.wait_ge(cnt_done, 1)
                link(V.tensor_scalar(nti[:], TOT, float(P - 1), float(P), ALU.add, ALU.max))
                link(V.tensor_scalar(nti[:], nti[:], P.bit_length() - 1, None, ALU.logical_shift_right))
                link(V.tensor_copy(nt[:], nti[:]))
                for e in range(E):
                    link(V.tensor_tensor(cum[:, e + 1:e + 2], cum[:, e:e + 1], nt[:, e:e + 1], ALU.add))
                start, end = cum[:, 0:E], cum[:, 1:E + 1]
                link(V.tensor_scalar(nt[:], start, float(P), None, ALU.mult))
                link(V.tensor_tensor(sc[:], CNT[:, 0:NT * E].rearrange("p (t e) -> p t e", t=NT), experts(nt[:]), ALU.add))
                for c in range(2):
                    link(V.tensor_tensor(tb[:], oh[c][:], sc[:], ALU.mult))
                    link(V.tensor_reduce(place[:, c, :], tb[:], AX.X, ALU.add))
                V.tensor_copy(keep.row[:], place[:])
                link(V.tensor_copy(slot_i[:], place[:]))
                V.tensor_scalar(row_i[:], slot_i[:], P - 1, None, ALU.bitwise_and)
                link(V.tensor_scalar(slot_i[:], slot_i[:], P.bit_length() - 1, None, ALU.logical_shift_right))
                V.tensor_copy(row_f[:], row_i[:])
                link(V.tensor_copy(slot_f[:], slot_i[:]))
                for c in range(2):
                    step(V.tensor_tensor(is_slot[:, c], slot_f[:, c, :].rearrange("p (t o) -> p t o", o=1).to_broadcast([P, NT, SLOTS]),
                                         grid[:].rearrange("p (o s) -> p o s", o=1).to_broadcast([P, NT, SLOTS]), ALU.is_equal),
                         "slot%d" % c)
                    for half in range(2):
                        part = slice(half * NT // 2, (half + 1) * NT // 2)
                        step(V.tensor_tensor(is_row[:, c, part],
                                             row_f[:, c, part].rearrange("p (t o) -> p t o", o=1).to_broadcast([P, NT // 2, P]),
                                             iota[:].rearrange("p (o n) -> p o n", o=1).to_broadcast([P, NT // 2, P]),
                                             ALU.is_equal), "row%d%d" % (c, half))
                low(0)
                link(V.tensor_tensor(ended[:], grid[:].rearrange("p (s o) -> p s o", o=1).to_broadcast([P, SLOTS, E]),
                                     end.rearrange("p (o e) -> p o e", o=1).to_broadcast([P, SLOTS, E]), ALU.is_ge))
                link(V.tensor_reduce(expert[:], ended[:], AX.X, ALU.add))
                link(V.tensor_scalar(keep.table[:, 0, :], expert[:], float(E - 1), None, ALU.min))
                link(V.tensor_scalar(keep.table[:, 1, :], keep.table[:, 0, :], 1, None, ALU.bitwise_and))
                V.tensor_copy(keep.ends[:], end)
                low(1)
                low(2)
                eng.wait_ge(idx_done, 1)
                V.tensor_copy(keep.token[:], IDX[:, 0:SLOTS]).then_inc(token_done, 1)
                low(3)

            @block.scalar
            def _(eng):
                eng.wait_ge(rt, at["logits"])
                nc.scalar.activation(sc[:], sc[:], ACT.Exp).then_inc(ex_done, 1)
                nc.scalar.copy(utri_r[:], utri[:]).then_inc(misc, 1)
                nc.scalar.copy(ones_r[:], ones[:]).then_inc(misc, 1)
                nc.scalar.activation(gt[:], gate[:], ACT.Tanh).then_inc(misc, 1)
                for g in range(LG):
                    eng.wait_ge(lt_done, g + 1)
                    nc.scalar.copy(keep.lt_hi[:, L * g:L * (g + 1)], LT[g % 3][:]).then_inc(lthi_done, 1)

            @block.gpsimd
            def _(eng):
                eng.wait_ge(rt, at["weights"])
                lora = lr[:, :, 0:ER].rearrange("p t (e r) -> p t e r", e=E)
                nc.gpsimd.tensor_tensor(lora, lora, wt[:].rearrange("p t (e o) -> p t e o", o=1).to_broadcast([P, NT, E, R]),
                                        ALU.mult).then_inc(lw_done, 1)
                for c in range(2):
                    eng.wait_ge(rt, at["slot%d" % c])
                    for half in range(2):
                        part = slice(half * NT // 2, (half + 1) * NT // 2)
                        nc.gpsimd.tensor_tensor(slot_number[:, c, part], is_slot[:, c, part],
                                                number[:, part].rearrange("p (t o) -> p t o", o=1).to_broadcast([P, NT // 2, SLOTS]),
                                                ALU.mult).then_inc(num_done, 1)
                eng.wait_ge(token_done, 1)
                for k in range(2):
                    rows.gather(eng, keep, normed_d, k)

            @block.tensor
            def _(eng):
                eng.wait_ge(misc, 3)
                eng.wait_ge(rt, at["chosen"])
                flat = chosen[:].rearrange("p t e -> p (t e)")
                nc.tensor.matmul(CNT[:, 0:NT * E], utri_r[:], flat, start=True, stop=False)
                grouped = CNT[:, 0:NT * E].rearrange("p (g t e) -> p g t e", t=GT, e=E)
                by_group = chosen[:].rearrange("p (g t) e -> p g t e", t=GT)
                for s in range(1, GT):
                    nc.tensor.matmul(grouped[:, :, s:GT, :], ones_r[:], by_group[:, :, 0:GT - s, :], start=False, stop=False)
                for s in range(1, NT // GT):
                    nc.tensor.matmul(grouped[:, s:NT // GT], ones_r[:],
                                     groups[:, 0:NT // GT - s, :].rearrange("p g (o e) -> p g o e", o=1)
                                     .to_broadcast([P, NT // GT - s, GT, E]), start=False, stop=s == NT // GT - 1)
                nc.tensor.matmul(TOT, ones_r[:], sums[:], start=True, stop=True).then_inc(cnt_done, 1)

                def turn(g):
                    if g > 2:
                        eng.wait_ge(ltlo_done, g - 2)
                    for t in range(L // P):
                        mm = nc.tensor.transpose(LT[g % 3][:, t * P:(t + 1) * P], lr[:, g * (L // P) + t, 0:ER], ident[:])
                    mm.then_inc(lt_done, 1)

                eng.wait_ge(lw_done, 1)
                for g in range(3):
                    turn(g)
                for c in range(2):
                    for half in range(2):
                        eng.wait_ge(num_done, 2 * c + half + 1)
                        eng.wait_ge(rt, at["row%d%d" % (c, half)])
                        for t in range(half * NT // 2, (half + 1) * NT // 2):
                            mm = nc.tensor.matmul(IDX[:, 0:SLOTS], is_row[:, c, t, :], slot_number[:, c, t, :],
                                                  start=c == 0 and t == 0, stop=c == 1 and t == NT - 1)
                mm.then_inc(idx_done, 1)
                turn(3)


def experts_on_slots(nc, keep, constants, weights, rows, base, x1_d, lb_d, whi_d, wlo_d, normed_d, made_d):
    ctx = ExitStack()
    with ctx:
        sb = lambda n, s, dt=F32: ctx.enter_context(nc.sbuf_tensor(n, s, dt))
        sem = lambda n: ctx.enter_context(nc.semaphore(n))
        ps = lambda n, s: ctx.enter_context(nc.psum_tensor(n, s, F32))
        ident = constants.ident
        xr, xr_in = rows.buffer, rows.landed
        xt_hi = [sb(f"xu_hi{p}", [P, NC, P], F32R) for p in range(2)]
        xt_lo = [sb(f"xu_lo{p}", [P, NC, P], F32R) for p in range(2)]
        h = [sb(f"h{p}", [P, F]) for p in range(2)]
        ht_hi = [sb(f"ht_hi{p}", [P, P], F32R) for p in range(2)]
        ht_lo = [sb(f"ht_lo{p}", [P, P], F32R) for p in range(2)]
        made = [sb(f"made{p}", [P, L]) for p in range(2)]
        XT = ps("XU", [P, L])
        GU = [ps(f"GU{p}", [P, HALF]) for p in range(2)]
        HT = ps("HT", [P, HALF])
        D = [ps(f"DD{c}", [P, HALF]) for c in range(2)]

        xt_ready, xhi_done, xlo_done = sem("xt_ready3"), sem("xhi_done3"), sem("xlo_done3")
        gu_ready = sem("gu_ready")
        silu_done, h_done = sem("silu_done"), sem("h_done")
        ht_ready, hhi_done, hlo_done = sem("ht_ready"), sem("hhi_done"), sem("hlo_done")
        d_ready = sem("d_ready")
        d_out = [sem(f"d_out{c}") for c in range(2)]
        made_out = [sem(f"made_out{p}") for p in range(2)]

        def table(kind, k):
            return keep.table[0:1, kind, bass.ds(k, 1)]

        with nc.Block() as block:

            @block.sync
            def _(eng):
                eng.dma_start(base.lb[:], lb_d).then_inc(base.lb_in, 16)
                early = NB - 2 * (WC // L)
                for x in range(2, E):
                    eng.wait_ge(d_ready, eng.value_load(keep.ends[0:1, x - 2:x - 1], min_val=1, max_val=SLOTS))
                    weights.load(eng, whi_d, wlo_d, x, singly=True)
                    base.load(eng, x1_d, range((x - 2) * early // (E - 2), (x - 1) * early // (E - 2)))
                eng.wait_ge(d_ready, eng.value_load(keep.ends[0:1, E - 2:E - 1], min_val=1, max_val=SLOTS))
                base.load(eng, x1_d, range(early, NB))

            @block.gpsimd
            def _(eng):
                def store(k):
                    eng.wait_ge(d_out[0], k + 1)
                    eng.wait_ge(d_out[1], k + 1)
                    eng.dma_start(made_d[k], made[k % 2][:]).then_inc(made_out[k % 2], 16)

                for k in range(SLOTS):
                    if k == 0:
                        eng.wait_ge(xt_ready, 1)
                        rows.gather(eng, keep, normed_d, 2)
                    if k + 3 < SLOTS:
                        eng.wait_ge(xt_ready, k + 2)
                        rows.gather(eng, keep, normed_d, k + 3)
                    if k:
                        store(k - 1)
                store(SLOTS - 1)
                for p in range(2):
                    eng.wait_ge(made_out[p], 16 * (SLOTS // 2))

            @block.scalar
            def _(eng):
                def high(k, p):
                    eng.wait_ge(xt_ready, k + 1)
                    if not (isinstance(k, int) and k < 2):
                        eng.wait_ge(gu_ready, k - 1)
                    nc.scalar.copy(xt_hi[p][:], XT[:].rearrange("p (c n) -> p c n", c=NC)).then_inc(xhi_done, 1)

                def slot(k, p, first=False, last=False):
                    if not last:
                        high(k + 1, 1 - p)
                    eng.wait_ge(gu_ready, k + 1)
                    if not (isinstance(k, int) and k < 2):
                        eng.wait_ge(ht_ready, k - 1)
                    nc.scalar.activation(h[p][:], GU[p][:, 0:F], ACT.Silu).then_inc(silu_done, 1)
                    if not first:
                        copy_out(k - 1, 1 - p)
                    eng.wait_ge(ht_ready, k + 1)
                    nc.scalar.copy(ht_hi[p][:], HT[:, 0:P]).then_inc(hhi_done, 1)

                def copy_out(k, p):
                    eng.wait_ge(d_ready, k + 1)
                    if not (isinstance(k, int) and k < 2):
                        eng.wait_ge(made_out[p], 8 * (k - p))
                    nc.scalar.copy(made[p][:, 0:HALF], D[0][:]).then_inc(d_out[0], 1)

                high(0, 0)
                eng.wait_ge(base.lb_in, 16)
                nc.scalar.copy(base.lb_hi[:], base.lb[:]).then_inc(base.lb_high, 1)
                slot(0, 0, first=True)
                slot(1, 1)
                with eng.Fori(1, SLOTS // 2 - 1) as j:
                    for p in range(2):
                        slot(2 * j + p, p)
                slot(SLOTS - 2, 0)
                slot(SLOTS - 1, 1, last=True)
                copy_out(SLOTS - 1, 1)

            @block.vector
            def _(eng):
                def lows(k, p):
                    eng.wait_ge(xhi_done, k + 1)
                    nc.vector.tensor_tensor(xt_lo[p][:], XT[:].rearrange("p (c n) -> p c n", c=NC),
                                            xt_hi[p][:].bitcast(F32), ALU.subtract).then_inc(xlo_done, 1)

                def copy_out(k, p):
                    eng.wait_ge(d_ready, k + 1)
                    if not (isinstance(k, int) and k < 2):
                        eng.wait_ge(made_out[p], 8 * (k - p))
                    nc.vector.tensor_copy(made[p][:, HALF:L], D[1][:]).then_inc(d_out[1], 1)

                def slot(k, p, first=False, last=False):
                    if not last:
                        lows(k + 1, 1 - p)
                    eng.wait_ge(silu_done, k + 1)
                    nc.vector.tensor_tensor(h[p][:], GU[p][:, F:2 * F], h[p][:], ALU.mult).then_inc(h_done, 1)
                    if not first:
                        copy_out(k - 1, 1 - p)
                    eng.wait_ge(hhi_done, k + 1)
                    nc.vector.tensor_tensor(ht_lo[p][:], HT[:, 0:P], ht_hi[p][:].bitcast(F32),
                                            ALU.subtract).then_inc(hlo_done, 1)

                lows(0, 0)
                slot(0, 0, first=True)
                eng.wait_ge(base.lb_high, 1)
                nc.vector.tensor_tensor(base.lb_lo[:], base.lb[:], base.lb_hi[:].bitcast(F32), ALU.subtract)
                slot(1, 1)
                with eng.Fori(1, SLOTS // 2 - 1) as j:
                    for p in range(2):
                        slot(2 * j + p, p)
                slot(SLOTS - 2, 0)
                slot(SLOTS - 1, 1, last=True)
                copy_out(SLOTS - 1, 1)

            @block.tensor
            def _(eng):
                def transposes(k, p):
                    eng.wait_ge(xr_in[p], 8 * (k - p) + 16)
                    if not (isinstance(k, int) and k < 1):
                        eng.wait_ge(xlo_done, k)
                    for c in range(NC):
                        mm = nc.tensor.transpose(XT[:, c * P:(c + 1) * P], xr[p][:, c * P:(c + 1) * P], ident[:])
                    mm.then_inc(xt_ready, 1)

                def first_product(k, p, odd):
                    eng.wait_ge(xlo_done, k + 1)
                    if not (isinstance(k, int) and k < 2):
                        eng.wait_ge(h_done, k - 1)
                    out = GU[p][:, 0:2 * F]
                    for c in range(NC):
                        cols = slice(c * 2 * F, (c + 1) * 2 * F)
                        wh = weights.hi[:, bass.ds(odd, 1), cols].rearrange("p o n -> p (o n)")
                        wl = weights.lo[:, bass.ds(odd, 1), cols].rearrange("p o n -> p (o n)")
                        nc.tensor.matmul(out, xt_hi[p][:, c, :], wh, start=c == 0, stop=False)
                        nc.tensor.matmul(out, xt_lo[p][:, c, :], wh, start=False, stop=False)
                        mm = nc.tensor.matmul(out, xt_hi[p][:, c, :], wl, start=False, stop=c == NC - 1)
                    mm.then_inc(gu_ready, 1)

                def second_product(k, p, odd):
                    eng.wait_ge(hlo_done, k + 1)
                    if not (isinstance(k, int) and k < 1):
                        eng.wait_ge(d_out[0], k)
                        eng.wait_ge(d_out[1], k)
                    for c in range(2):
                        cols = slice(NC * 2 * F + c * HALF, NC * 2 * F + (c + 1) * HALF)
                        wh = weights.hi[:, bass.ds(odd, 1), cols].rearrange("p o n -> p (o n)")
                        wl = weights.lo[:, bass.ds(odd, 1), cols].rearrange("p o n -> p (o n)")
                        nc.tensor.matmul(D[c][:], ht_hi[p][:], wh, start=True, stop=False)
                        nc.tensor.matmul(D[c][:], ht_lo[p][:], wh, start=False, stop=False)
                        mm = nc.tensor.matmul(D[c][:], ht_hi[p][:], wl, start=False, stop=True)
                    mm.then_inc(d_ready, 1)

                def turn(k, p):
                    eng.wait_ge(h_done, k + 1)
                    if not (isinstance(k, int) and k < 1):
                        eng.wait_ge(hlo_done, k)
                    nc.tensor.transpose(HT[:, 0:P], h[p][:], ident[:]).then_inc(ht_ready, 1)

                expert = [eng.alloc_register(f"expert{p}") for p in range(2)]
                parity = [eng.alloc_register(f"parity{p}") for p in range(2)]
                loaded = eng.alloc_register("loaded")

                def read_table(k, p):
                    eng.reg_load(loaded, table(0, k))
                    eng.reg_alu(expert[p], loaded, 0, ALU.max)
                    eng.reg_load(parity[p], table(1, k))

                def slot(k, p, first=False, last=False):
                    if not last:
                        transposes(k + 1, 1 - p)
                    e = eng.snap(expert[p], min_val=0, max_val=E - 1)
                    odd = eng.snap(parity[p], min_val=0, max_val=1)
                    eng.wait_ge(weights.landed, LANDED * e + LANDED)
                    first_product(k, p, odd)
                    if not first:
                        second_product(k - 1, 1 - p, eng.snap(parity[1 - p], min_val=0, max_val=1))
                    if not last:
                        read_table(k + 1, 1 - p)
                    turn(k, p)

                read_table(0, 0)
                transposes(0, 0)
                slot(0, 0, first=True)
                slot(1, 1)
                with eng.Fori(1, SLOTS // 2 - 1) as j:
                    for p in range(2):
                        slot(2 * j + p, p)
                slot(SLOTS - 2, 0)
                slot(SLOTS - 1, 1, last=True)
                second_product(SLOTS - 1, 1, eng.snap(parity[1], min_val=0, max_val=1))


def combine(nc, keep, base, x1_d, made_d, out_d):
    ctx = ExitStack()
    with ctx:
        sb = lambda n, s, dt=F32: ctx.enter_context(nc.sbuf_tensor(n, s, dt))
        sem = lambda n: ctx.enter_context(nc.semaphore(n))
        DEPTH = 3
        lb_hi, lb_lo = base.lb_hi, base.lb_lo
        pick = [[sb(f"pick{c}{p}", [P, L]) for p in range(DEPTH)] for c in range(2)]
        D = [ctx.enter_context(nc.psum_tensor(f"DL{p}", [P, L], F32)) for p in range(DEPTH)]
        pick_in = [sem(f"pick_in{p}") for p in range(DEPTH)]
        d_ready = sem("d_ready4")
        added = sem("added")
        out_done = sem("out_done")

        with nc.Block() as block:

            @block.sync
            def _(eng):
                for i in range(NT):
                    if i < NT - NB:
                        eng.dma_start(base.at[NB + i], x1_d[NB + i]).then_inc(base.late[i], 16)
                    eng.wait_ge(added, 3 * i + 3)
                    eng.dma_start(out_d[i], base.at[i]).then_inc(out_done, 16)
                eng.wait_ge(out_done, 16 * NT)

            @block.gpsimd
            def _(eng):
                for i in range(NT):
                    p = i % DEPTH
                    if i >= DEPTH:
                        eng.wait_ge(added, 3 * (i - DEPTH) + 3)
                    for c in range(2):
                        eng.indirect_dma_start(out=pick[c][p][:], out_offset=None, in_=made_d,
                                               in_offset=bass.IndirectOffsetOnAxis(ap=keep.row[:, c, i:i + 1], axis=0)) \
                            .then_inc(pick_in[p], 16)

            @block.vector
            def _(eng):
                for i in range(NT):
                    p, acc = i % DEPTH, base.at[i]
                    if i >= NB:
                        eng.wait_ge(base.late[i - NB], 16)
                    eng.wait_ge(d_ready, i + 1)
                    nc.vector.tensor_tensor(acc, D[p][:], acc, ALU.add).then_inc(added, 1)
                    eng.wait_ge(pick_in[p], 32 * (i // DEPTH) + 32)
                    for c in range(2):
                        eng.wait_ge(added, 3 * i + 1 + c)
                        nc.vector.scalar_tensor_tensor(out=acc, in0=pick[c][p][:], scalar=keep.w[:, c, i:i + 1],
                                                       in1=acc, op0=ALU.mult, op1=ALU.add).then_inc(added, 1)

            @block.tensor
            def _(eng):
                for i in range(NT):
                    p = i % DEPTH
                    if i >= DEPTH:
                        eng.wait_ge(added, 3 * (i - DEPTH) + 1)
                    th, tl = keep.lt_hi[:, i * P:(i + 1) * P], keep.lt_lo[:, i * P:(i + 1) * P]
                    for c in range(2):
                        cols = slice(c * HALF, (c + 1) * HALF)
                        nc.tensor.matmul(D[p][:, cols], th, lb_hi[:, cols], start=True, stop=False)
                        nc.tensor.matmul(D[p][:, cols], tl, lb_hi[:, cols], start=False, stop=False)
                        mm = nc.tensor.matmul(D[p][:, cols], th, lb_lo[:, cols], start=False, stop=True)
                    mm.then_inc(d_ready, 1)


def build(nc, x, c, k, dskip, g1, g2, ident, ag, w, lb, order, utri, ones, iota, grid, number, out):
    dram = lambda n, s: nc.dram_tensor(n, s, F32).ap()
    khi, klo = dram("khi", [NH, KW]), dram("klo", [NH, KW])
    whi, wlo = dram("whi", [NT, P, WQ]), dram("wlo", [NT, P, WQ])
    x1, normed = dram("x1", [NT, P, L]), dram("normed", [NT, P, L])
    made = dram("made_rows", [SLOTS, P, L])
    with ExitStack() as ctx:
        lr = ctx.enter_context(nc.sbuf_tensor("lr", [P, NT, AC], F32))
        constants = Constants(nc, ctx, g1, g2, ident, order, utri, ones, iota, grid, number)
        attend(nc, lr, constants, x, c, k, dskip, ag, w, khi, klo, x1, normed, whi, wlo)
        normed = normed.rearrange("t p l -> (t p) l")
        keep, weights, rows = Chosen(nc, ctx), Weights(nc, ctx), Rows(nc, ctx)
        route_tokens(nc, keep, weights, rows, lr, constants, normed, whi, wlo)
        base = Base(nc, ctx, lr, weights, rows)
        experts_on_slots(nc, keep, constants, weights, rows, base, x1, lb, whi, wlo, normed, made)
        combine(nc, keep, base, x1, made.rearrange("s p l -> (s p) l"), out)


def kernel(**inputs):
    import numpy as np
    import concourse.bacc as bacc
    from concourse.bass_utils import run_bass_kernel_spmd
    a = {n: np.asarray(v) for n, v in inputs.items()}

    def rows(t):
        return np.ascontiguousarray(t.reshape(B, NT, CT, L).transpose(1, 2, 0, 3)).reshape(NT, P, L)

    def model_major(t):
        return t.reshape(t.shape[0], t.shape[1], NC, P).transpose(0, 3, 2, 1)

    c = a["ctx_2048"].reshape(B, NT, HT, HD, NC, P).transpose(1, 5, 2, 4, 3, 0)[:, ::-1].reshape(NT, P, HT, NC, IB)
    k = a["L0_xattn_ssm_kernel"]
    arrays = {
        "x": rows(a["x"]),
        "c": np.ascontiguousarray(np.concatenate([c, c[..., :IB // 2]], axis=-1)),
        "k": np.ascontiguousarray(np.pad(k, ((0, 0), (P - 1, 1)))),
        "dskip": np.ascontiguousarray(a["L0_xattn_D"].reshape(NH, 1)),
        "g1": np.ascontiguousarray(np.broadcast_to(a["g_xattn"].reshape(1, 1), (P, 1))),
        "g2": np.ascontiguousarray(np.broadcast_to(a["g_ffn"].reshape(1, 1), (P, 1))),
        "ident": np.eye(P, dtype=np.float32),
        "ag": np.ascontiguousarray(np.concatenate([model_major(a["L0_ffn_lora_A"].reshape(1, ER, L))[0],
                                                   a["L0_ffn_G"].reshape(NC, P, E).transpose(1, 0, 2)], axis=2)),
        "w": np.ascontiguousarray(np.concatenate([
            np.concatenate([model_major(a["L0_ffn_gate_w"]), model_major(a["L0_ffn_up_w"])], axis=3).reshape(E, P, -1),
            a["L0_ffn_down_w"].transpose(0, 2, 1)], axis=2).reshape(E, P, NT // E, WQ).transpose(0, 2, 1, 3)).reshape(NT, P, WQ),
        "lb": np.ascontiguousarray(a["L0_ffn_lora_B"].transpose(0, 2, 1).reshape(ER, L)),
        "order": np.ascontiguousarray(np.broadcast_to(np.arange(E, 0, -1, dtype=np.float32), (P, E))),
        "utri": np.triu(np.ones((P, P), np.float32), 1),
        "ones": np.ones((P, P), np.float32),
        "iota": np.ascontiguousarray(np.broadcast_to(np.arange(P, dtype=np.float32), (P, P))),
        "grid": np.ascontiguousarray(np.broadcast_to(np.arange(SLOTS, dtype=np.float32), (P, SLOTS))),
        "number": np.ascontiguousarray(np.arange(TOKENS, dtype=np.float32).reshape(NT, P).T),
    }
    nc = bacc.Bacc("TRN2", target_bir_lowering=False, num_devices=1)
    ins = [nc.dram_tensor("in_" + n, v.shape, mybir.dt.from_np(v.dtype), kind="ExternalInput").ap() for n, v in arrays.items()]
    out = nc.dram_tensor("out", (NT, P, L), F32, kind="ExternalOutput").ap()
    build(nc, *ins, out)
    r = run_bass_kernel_spmd(nc, [{"in_" + n: v for n, v in arrays.items()}], core_ids=[0])
    y = r.results[0]["out"]
    return np.ascontiguousarray(y.reshape(NT, CT, B, L).transpose(2, 0, 1, 3)).reshape(B, CH, L)
```
